# Optimizing a Trainium2 kernel written in Bass

```python
import numpy as np
import jax
import jax.numpy as jnp

def _softmax(x, axis=-1):
    return jax.nn.softmax(x, axis=axis)

def _gelu(x):
    return jax.nn.gelu(x, approximate=True)

def _silu(x):
    return jax.nn.silu(x)

def _sigmoid(x):
    return jax.nn.sigmoid(x)

def _layernorm(x, axis=-1, eps=1e-05):
    m = jnp.mean(x, axis=axis, keepdims=True)
    v = jnp.var(x, axis=axis, keepdims=True)
    return (x - m) / jnp.sqrt(v + eps)

def _scatter_add(tgt, idx, src, axis=0):
    return tgt.at[idx].add(src)

def _segment_sum(src, seg, n):
    return jax.ops.segment_sum(src, seg, n)
kernel_name = 'mk_flamingo_gated_d2_seqx_r8_f9cc7d'

def setup_inputs(seed: int=0):
    np.random.seed(seed)
    _w = jnp.asarray

    def _rec_inputs():
        import jax
        import jax.numpy as jnp
        _rk = jax.random.key(seed)
        x = 7.22e-05 + 1 * jax.random.normal(jax.random.fold_in(_rk, 1), (16, 64, 128), jnp.float32)
        _lenS = 64 - jax.random.randint(jax.random.fold_in(_rk, 7), (16,), 0, max(1, 64 // 4) + 1, jnp.int32)
        _lenS2 = 64 - jax.random.randint(jax.random.fold_in(_rk, 8), (16,), 0, max(1, 64 // 4) + 1, jnp.int32)
        _ctx_1024P = jax.random.normal(jax.random.fold_in(_rk, 11), (16, 16, 128), jnp.float32)
        _ctx_1024c = jax.random.dirichlet(jax.random.fold_in(_rk, 511), 0.3 * jnp.ones((16,), jnp.float32), (16, 64))
        _ctx_1024t = jnp.einsum('bsk,bkd->bsd', _ctx_1024c, _ctx_1024P)
        _ctx_1024t = _ctx_1024t * jax.lax.rsqrt(jnp.mean(jnp.square(_ctx_1024t)) + 1e-12) * 0.953939
        ctx_1024 = 4.13588e-05 + 0.999923 * (_ctx_1024t + 0.3 * jax.random.normal(jax.random.fold_in(_rk, 611), (16, 64, 128), jnp.float32))
        fside_1xSxS2_0 = 0.000675642 + 1.00031 * jax.random.normal(jax.random.fold_in(_rk, 12), (1, 64, 64), jnp.float32)
        _validS = jnp.arange(64)[None, :] < _lenS[:, None]
        _validS2 = jnp.arange(64)[None, :] < _lenS2[:, None]
        _causal = jnp.tril(jnp.ones((64, 64), dtype=bool))
        mask_BxS2_bk0 = jnp.logical_not(jnp.broadcast_to(_validS2[:, :], (16, 64)))
        _g = jax.random.normal(jax.random.fold_in(_rk, 9001), (2, 2), jnp.float32)
        _g = jnp.sign(_g) * jnp.maximum(jnp.abs(_g), 1.0) + (_g == 0) * 1.0
        g_xattn = _g[0]
        g_ffn = _g[1]
        return (x, ctx_1024, fside_1xSxS2_0, mask_BxS2_bk0, g_xattn, g_ffn)
    x, ctx_1024, fside_1xSxS2_0, mask_BxS2_bk0, g_xattn, g_ffn = _rec_inputs()

    def _L0_xattn_setup():
        import jax, jax.numpy as jnp
        import numpy as np
        D_MODEL = 128
        NUM_HEADS = 16
        D_K = D_MODEL // NUM_HEADS
        key = jax.random.key(seed)
        ks = jax.random.split(key, 8)
        B, S, D = (4, 256, D_MODEL)
        scale = 1.0 / np.sqrt(D)
        return {'query': jax.random.normal(ks[0], (B, S, D), dtype=jnp.float32), 'key': jax.random.normal(ks[1], (B, S, D), dtype=jnp.float32), 'value': jax.random.normal(ks[2], (B, S, D), dtype=jnp.float32), 'Wq': jax.random.normal(ks[3], (D, D), dtype=jnp.float32) * scale, 'bq': jnp.zeros((D,), dtype=jnp.float32), 'Wk': jax.random.normal(ks[4], (D, D), dtype=jnp.float32) * scale, 'bk': jnp.zeros((D,), dtype=jnp.float32), 'Wv': jax.random.normal(ks[5], (D, D), dtype=jnp.float32) * scale, 'bv': jnp.zeros((D,), dtype=jnp.float32), 'Wo': jax.random.normal(ks[6], (D, D), dtype=jnp.float32) * scale, 'bo': jnp.zeros((D,), dtype=jnp.float32)}
    _L0_xattn_all = _L0_xattn_setup()
    _L0_xattn_in = {k: v for k, v in _L0_xattn_all.items() if k in ('Wq', 'bq', 'Wk', 'bk', 'Wv', 'bv', 'Wo', 'bo')}
    del _L0_xattn_all

    def _L0_ffn_setup():
        import jax, jax.numpy as jnp
        import numpy as np
        B, S, H, F, E = (1, 256, 128, 256, 8)

        def _swiglu(x, wg, wu, wd):
            return jax.nn.silu(x @ wg.T) * (x @ wu.T) @ wd.T
        key = jax.random.key(seed)
        ks = jax.random.split(key, 8)
        sc = 1.0 / np.sqrt(H)
        scf = 1.0 / np.sqrt(F)
        return {'hidden_states': jax.random.normal(ks[0], (B, S, H), jnp.float32), 'gate_w': jax.random.normal(ks[1], (E, H), jnp.float32) * sc, 'shared_gate': jax.random.normal(ks[2], (F, H), jnp.float32) * sc, 'shared_up': jax.random.normal(ks[3], (F, H), jnp.float32) * sc, 'shared_down': jax.random.normal(ks[4], (H, F), jnp.float32) * scf, 'r_gate': jax.random.normal(ks[5], (E, F, H), jnp.float32) * sc, 'r_up': jax.random.normal(ks[6], (E, F, H), jnp.float32) * sc, 'r_down': jax.random.normal(ks[7], (E, H, F), jnp.float32) * scf}
    _L0_ffn_all = _L0_ffn_setup()
    _L0_ffn_in = {k: v for k, v in _L0_ffn_all.items() if k in ('gate_w', 'shared_gate', 'shared_up', 'shared_down', 'r_gate', 'r_up', 'r_down')}
    del _L0_ffn_all

    def _L1_xattn_setup():
        import jax, jax.numpy as jnp
        import numpy as np
        EMBED_DIM = 128
        NUM_HEADS = 16
        HEAD_DIM = EMBED_DIM // NUM_HEADS
        SCALING = float(HEAD_DIM * 1.0) ** (-0.5)
        NEG_INF = float(np.finfo(np.float32).min)
        key = jax.random.key(seed)
        ks = jax.random.split(key, 8)
        B, T, S, E = (2, 256, 256, EMBED_DIM)
        return {'query': jax.random.normal(ks[0], (B, T, E), jnp.float32), 'key': jax.random.normal(ks[1], (B, S, E), jnp.float32), 'value': jax.random.normal(ks[2], (B, S, E), jnp.float32), 'attn_bias': jax.random.normal(ks[3], (1, T, S), jnp.float32), 'key_padding_mask': jax.random.randint(ks[4], (B, S), 0, 2).astype(bool), 'in_proj_w': jax.random.normal(ks[5], (3 * E, E), jnp.float32) * E ** (-0.5), 'in_proj_b': jnp.zeros((3 * E,), jnp.float32), 'out_proj_w': jax.random.normal(ks[6], (E, E), jnp.float32) * E ** (-0.5), 'out_proj_b': jnp.zeros((E,), jnp.float32)}
    _L1_xattn_all = _L1_xattn_setup()
    _L1_xattn_in = {k: v for k, v in _L1_xattn_all.items() if k in ('in_proj_w', 'in_proj_b', 'out_proj_w', 'out_proj_b')}
    del _L1_xattn_all

    def _L1_ffn_setup():
        import jax, jax.numpy as jnp
        import numpy as np
        D_MODEL, D_FF, NUM_EXPERTS, RANK, TOP_K = (128, 512, 8, 16, 2)
        B, S = (8, 256)

        def _expert_ffn(h, wi_w, wo_w, A, Bm):
            inter = jnp.einsum('bsd,fd->bsf', h, wi_w)
            lora = jnp.einsum('bsr,fr->bsf', jnp.einsum('bsd,rd->bsr', h, A), Bm)
            inter = jax.nn.relu(inter + lora)
            return jnp.einsum('bsf,df->bsd', inter, wo_w)
        key = jax.random.key(seed)
        ks = jax.random.split(key, 8)
        hidden_states = jax.random.normal(ks[0], (B, S, D_MODEL), dtype=jnp.float32)
        wi_w = jax.random.normal(ks[1], (D_FF, D_MODEL), dtype=jnp.float32) * (1.0 / np.sqrt(D_MODEL))
        wo_w = jax.random.normal(ks[2], (D_MODEL, D_FF), dtype=jnp.float32) * (1.0 / np.sqrt(D_FF))
        lora_As = jax.random.uniform(ks[3], (NUM_EXPERTS, RANK, D_MODEL), dtype=jnp.float32, minval=-1.0, maxval=1.0) / np.sqrt(D_MODEL)
        lora_Bs = jax.random.normal(ks[4], (NUM_EXPERTS, D_FF, RANK), dtype=jnp.float32) * 0.02
        top_k_indices = jnp.arange(TOP_K, dtype=jnp.int32)
        top_k_values = jax.random.uniform(ks[5], (TOP_K,), dtype=jnp.float32)
        return {'hidden_states': hidden_states, 'wi_w': wi_w, 'wo_w': wo_w, 'lora_As': lora_As, 'lora_Bs': lora_Bs, 'top_k_indices': top_k_indices, 'top_k_values': top_k_values}
    _L1_ffn_all = _L1_ffn_setup()
    _L1_ffn_in = {k: v for k, v in _L1_ffn_all.items() if k in ('wi_w', 'wo_w', 'lora_As', 'lora_Bs', 'top_k_indices', 'top_k_values')}
    del _L1_ffn_all
    return {'x': x, 'ctx_1024': ctx_1024, 'fside_1xSxS2_0': fside_1xSxS2_0, 'mask_BxS2_bk0': mask_BxS2_bk0, 'g_xattn': g_xattn, 'g_ffn': g_ffn, 'L0_xattn_Wq': _L0_xattn_in['Wq'], 'L0_xattn_bq': _L0_xattn_in['bq'], 'L0_xattn_Wk': _L0_xattn_in['Wk'], 'L0_xattn_bk': _L0_xattn_in['bk'], 'L0_xattn_Wv': _L0_xattn_in['Wv'], 'L0_xattn_bv': _L0_xattn_in['bv'], 'L0_xattn_Wo': _L0_xattn_in['Wo'], 'L0_xattn_bo': _L0_xattn_in['bo'], 'L0_ffn_gate_w': _L0_ffn_in['gate_w'], 'L0_ffn_shared_gate': _L0_ffn_in['shared_gate'], 'L0_ffn_shared_up': _L0_ffn_in['shared_up'], 'L0_ffn_shared_down': _L0_ffn_in['shared_down'], 'L0_ffn_r_gate': _L0_ffn_in['r_gate'], 'L0_ffn_r_up': _L0_ffn_in['r_up'], 'L0_ffn_r_down': _L0_ffn_in['r_down'], 'L1_xattn_in_proj_w': _L1_xattn_in['in_proj_w'], 'L1_xattn_in_proj_b': _L1_xattn_in['in_proj_b'], 'L1_xattn_out_proj_w': _L1_xattn_in['out_proj_w'], 'L1_xattn_out_proj_b': _L1_xattn_in['out_proj_b'], 'L1_ffn_wi_w': _L1_ffn_in['wi_w'], 'L1_ffn_wo_w': _L1_ffn_in['wo_w'], 'L1_ffn_lora_As': _L1_ffn_in['lora_As'], 'L1_ffn_lora_Bs': _L1_ffn_in['lora_Bs'], 'L1_ffn_top_k_indices': _L1_ffn_in['top_k_indices'], 'L1_ffn_top_k_values': _L1_ffn_in['top_k_values']}

def reference(x, ctx_1024, fside_1xSxS2_0, mask_BxS2_bk0, g_xattn, g_ffn, L0_xattn_Wq, L0_xattn_bq, L0_xattn_Wk, L0_xattn_bk, L0_xattn_Wv, L0_xattn_bv, L0_xattn_Wo, L0_xattn_bo, L0_ffn_gate_w, L0_ffn_shared_gate, L0_ffn_shared_up, L0_ffn_shared_down, L0_ffn_r_gate, L0_ffn_r_up, L0_ffn_r_down, L1_xattn_in_proj_w, L1_xattn_in_proj_b, L1_xattn_out_proj_w, L1_xattn_out_proj_b, L1_ffn_wi_w, L1_ffn_wo_w, L1_ffn_lora_As, L1_ffn_lora_Bs, L1_ffn_top_k_indices, L1_ffn_top_k_values):
    import jax
    import jax.numpy as jnp

    def _L0_xattn_ref(query, key, value, Wq, bq, Wk, bk, Wv, bv, Wo, bo):
        import jax, jax.numpy as jnp
        import numpy as np
        D_MODEL = 128
        NUM_HEADS = 16
        D_K = D_MODEL // NUM_HEADS
        B, S, D = query.shape
        H, dk = (NUM_HEADS, D_K)

        def proj(x, W, b):
            y = jnp.einsum('bsd,ed->bse', x, W) + b
            return y.reshape(B, -1, H, dk).transpose(0, 2, 1, 3)
        Q = proj(query, Wq, bq)
        K = proj(key, Wk, bk)
        V = proj(value, Wv, bv)
        scores = jnp.einsum('bhqd,bhkd->bhqk', Q, K) / np.sqrt(dk).astype(jnp.float32)
        attn = jax.nn.softmax(scores, axis=-1)
        out = jnp.einsum('bhqk,bhkd->bhqd', attn, V)
        out = out.transpose(0, 2, 1, 3).reshape(B, -1, D)
        return jnp.einsum('bsd,ed->bse', out, Wo) + bo

    def _L0_ffn_ref(hidden_states, gate_w, shared_gate, shared_up, shared_down, r_gate, r_up, r_down):
        import jax, jax.numpy as jnp
        import numpy as np
        B, S, H, F, E = (1, 256, 128, 256, 8)

        def _swiglu(x, wg, wu, wd):
            return jax.nn.silu(x @ wg.T) * (x @ wu.T) @ wd.T
        b, s, h = hidden_states.shape
        x = hidden_states.reshape(-1, h)
        shared_out = _swiglu(x, shared_gate, shared_up, shared_down)
        logits = x @ gate_w.T
        top_id = jnp.argmax(logits, axis=-1)
        score = jax.nn.sigmoid(jnp.max(logits, axis=-1))
        xs = x * score[:, None]

        def body(acc, ws):
            wg, wu, wd, e = ws
            xe = jnp.where((top_id == e)[:, None], xs, 0.0)
            return (acc + _swiglu(xe, wg, wu, wd), None)
        acc0 = jnp.zeros_like(x)
        routed_out, _ = jax.lax.scan(body, acc0, (r_gate, r_up, r_down, jnp.arange(E)))
        return (shared_out + routed_out).reshape(b, s, h)

    def _L1_xattn_ref(query, key, value, attn_bias, key_padding_mask, in_proj_w, in_proj_b, out_proj_w, out_proj_b):
        import jax, jax.numpy as jnp
        import numpy as np
        EMBED_DIM = 128
        NUM_HEADS = 16
        HEAD_DIM = EMBED_DIM // NUM_HEADS
        SCALING = float(HEAD_DIM * 1.0) ** (-0.5)
        NEG_INF = float(np.finfo(np.float32).min)
        B, T, E = query.shape
        S = key.shape[1]
        H, D = (NUM_HEADS, HEAD_DIM)
        w_q, w_k, w_v = (in_proj_w[:E], in_proj_w[E:2 * E], in_proj_w[2 * E:])
        b_q, b_k, b_v = (in_proj_b[:E], in_proj_b[E:2 * E], in_proj_b[2 * E:])
        q = (query @ w_q.T + b_q).reshape(B, T, H, D)
        k = (key @ w_k.T + b_k).reshape(B, S, H, D)
        v = (value @ w_v.T + b_v).reshape(B, S, H, D)
        scores = jnp.einsum('bthd,bshd->bhts', q * SCALING, k)
        scores = scores + attn_bias[None]
        scores = jnp.where(key_padding_mask[:, None, None, :], NEG_INF, scores)
        attn = jax.nn.softmax(scores, axis=-1)
        out = jnp.einsum('bhts,bshd->bthd', attn, v).reshape(B, T, E)
        return out @ out_proj_w.T + out_proj_b

    def _L1_ffn_ref(hidden_states, wi_w, wo_w, lora_As, lora_Bs, top_k_indices, top_k_values):
        import jax, jax.numpy as jnp
        import numpy as np
        D_MODEL, D_FF, NUM_EXPERTS, RANK, TOP_K = (128, 512, 8, 16, 2)
        B, S = (8, 256)

        def _expert_ffn(h, wi_w, wo_w, A, Bm):
            inter = jnp.einsum('bsd,fd->bsf', h, wi_w)
            lora = jnp.einsum('bsr,fr->bsf', jnp.einsum('bsd,rd->bsr', h, A), Bm)
            inter = jax.nn.relu(inter + lora)
            return jnp.einsum('bsf,df->bsd', inter, wo_w)
        out = jnp.zeros_like(hidden_states)
        for k in range(top_k_values.shape[0]):
            A = jnp.take(lora_As, top_k_indices[k], axis=0)
            Bm = jnp.take(lora_Bs, top_k_indices[k], axis=0)
            out = out + top_k_values[k] * _expert_ffn(hidden_states, wi_w, wo_w, A, Bm)
        return out
    x = x + jnp.tanh(g_xattn[0]) * _L0_xattn_ref(_layernorm(x, axis=-1), ctx_1024, ctx_1024, L0_xattn_Wq, L0_xattn_bq, L0_xattn_Wk, L0_xattn_bk, L0_xattn_Wv, L0_xattn_bv, L0_xattn_Wo, L0_xattn_bo)
    x = x + jnp.tanh(g_ffn[0]) * _L0_ffn_ref(_layernorm(x, axis=-1), L0_ffn_gate_w, L0_ffn_shared_gate, L0_ffn_shared_up, L0_ffn_shared_down, L0_ffn_r_gate, L0_ffn_r_up, L0_ffn_r_down)
    x = x + jnp.tanh(g_xattn[1]) * _L1_xattn_ref(_layernorm(x, axis=-1), ctx_1024, ctx_1024, fside_1xSxS2_0, mask_BxS2_bk0, L1_xattn_in_proj_w, L1_xattn_in_proj_b, L1_xattn_out_proj_w, L1_xattn_out_proj_b)
    x = x + jnp.tanh(g_ffn[1]) * _L1_ffn_ref(_layernorm(x, axis=-1), L1_ffn_wi_w, L1_ffn_wo_w, L1_ffn_lora_As, L1_ffn_lora_Bs, L1_ffn_top_k_indices, L1_ffn_top_k_values)
    return x

_drawn_inputs = setup_inputs


def setup_inputs(seed=0):
    import zlib

    import numpy as np

    out = dict(_drawn_inputs(seed))
    spreads = {'g_ffn': (-1.0, 0.2),
     'L0_xattn_bq': (0.0, 0.1),
     'L0_xattn_bk': (0.0, 0.8),
     'L0_xattn_bv': (0.0, 0.1),
     'L0_xattn_bo': (0.0, 0.1),
     'L1_xattn_in_proj_b': (0.0, 0.1),
     'L1_xattn_out_proj_b': (0.0, 0.1)}
    factors = {'L1_ffn_lora_As': 3.47, 'L1_ffn_lora_Bs': 3.47, 'L1_ffn_top_k_values': 8.0}
    for name, (base, spread) in spreads.items():
        noise = np.random.default_rng([zlib.crc32(name.encode()), seed]).standard_normal(out[name].shape)
        drawn = base * np.exp(spread * noise) if base else spread * noise
        out[name] = jnp.asarray(drawn.astype(out[name].dtype))
    for name, factor in factors.items():
        out[name] = (out[name] * factor).astype(out[name].dtype)
    return out
```

```python
from contextlib import ExitStack

import concourse.bass as bass
from concourse import mybir

F32 = mybir.dt.float32
BF16 = mybir.dt.bfloat16
U32 = mybir.dt.uint32
I32 = mybir.dt.int32
ALU = mybir.AluOpType
ACT = mybir.ActivationFunctionType
AX = mybir.AxisListType

B, S, D = 16, 64, 128
H, DK = 16, 8
T = B * S
P = 128
TILES = T // P
CH = 2
TPC = TILES // CH
TC = T // CH
PAIRS = B // 2
UNITS = PAIRS * 2
HH = H // 2
HP = H // 2
E, F = 8, 256
SLOT_TILES = TILES + E - 1
ROW = D + 4
F1 = 512
FB1 = F1 // P
RANK, TOPK = 16, 2
SCALE = DK ** -0.5
EPS = 1e-5
NEG = -3.4028234663852886e38

WK, WV, BK, BV, BQ = 0, D, 2 * D, 2 * D + 1, 2 * D + 2
WQ, WO, WGATE = 2 * D + 3, 3 * D + 3, 4 * D + 3
ATT_COLS = 4 * D + 3 + E
ID, ONESX, W8, THR, TRI8, JT = 0, 128, 192, 200, 208, 272
CONST_COLS = JT + 16
BO0, BO1, GATES, TOPV = 0, D, 2 * D, 2 * D + 4
ROW_COLS = 2 * D + 4 + TOPK


def last_bcast(ap, n):
    return bass.AP(ap.tensor, ap.offset, [list(d) for d in ap.ap] + [[0, n]])


def mid_bcast(ap, n):
    dims = [list(d) for d in ap.ap]
    return bass.AP(ap.tensor, ap.offset, dims[:1] + [[0, n]] + dims[1:])


def build(nc, x_in, ctx_in, att0, att1, consts, constb, rows, shared, rgu, rdn, ffn1, lora, topi,
          bias, mask, tok_ids, slot_init, out):
    with ExitStack() as ctx:
        def sb(name, shape, dt=F32):
            return ctx.enter_context(nc.sbuf_tensor(name, shape, dt))

        def sem(name):
            return ctx.enter_context(nc.semaphore(name))

        bank = [ctx.enter_context(nc.psum_tensor(f"bank{i}", [P, 512], F32)) for i in range(8)]
        xs_dram = nc.dram_tensor("sorted_rows", [SLOT_TILES * P, ROW], F32).ap()
        y_dram = nc.dram_tensor("routed_rows", [T, D], F32).ap()

        ctxT = sb("ctxT", [P, T])
        wat = [sb("wat0", [P, ATT_COLS]), sb("wat1", [P, ATT_COLS])]
        cst = sb("cst", [P, CONST_COLS])
        cstb = sb("cstb", [P, 2 * P], BF16)
        row = sb("row", [P, ROW_COLS])
        wsh = sb("wsh", [P, 3 * F])
        wgu = sb("wgu", [P, E * 2 * F])
        wdn = sb("wdn", [P, E * 2 * D])
        wf1 = sb("wf1", [P, 2 * F1])
        tki = sb("tki", [1, TOPK], I32)
        msk = sb("msk", [P, PAIRS, S], mybir.dt.uint8)
        bia = sb("bia", [P, S])
        bm = wsh[:, 0:PAIRS * S].rearrange("p (a k) -> p a k", a=PAIRS)
        tg = sb("tg", [P, 4])
        xr = [sb(f"xr{i}", [P, TILES, D]) for i in range(2)]
        xres = [xr[0], xr[1], xr[0], xr[1], xr[0]]
        xb = sb("xb", [P, TILES, D])
        xn = sb("xn", [P, TILES, D])
        xnT = sb("xnT", [P, T])
        st = sb("st", [P, TILES, 6])
        mv = sb("mv", [P, TILES, 2])
        ve = sb("ve", [P, TILES])
        nhalf = sb("nhalf", [P, TILES])
        rstd = sb("rstd", [P, TILES])
        nmr = sb("nmr", [P, TILES])
        KT = sb("KT", [P, T])
        QT = sb("QT", [P, T])
        lor = QT[:, 0:D + F1]
        oT = sb("oT", [P, T])
        Kx = sb("Kx", [P, H, T])
        Vx = sb("Vx", [P, B, HP, 32])
        Sa = sb("Sa", [P, 2, HH * S])
        Sx = sb("Sx", [P, 2, HH * S])
        Pe = sb("Pe", [P, 3, HH * S])
        mx = sb("mx", [P, 4, HH])
        bvb = sb("bvb", [P, D])
        bo = sb("bo", [P, D])
        big = sb("big", [P, HP * T])
        PT = big[:, :].rearrange("p (a t) -> p a t", a=HP)
        hsT = big[:, 0:2 * T].rearrange("p (f t) -> p f t", f=2)
        XS = big[:, 2 * T:2 * T + SLOT_TILES * ROW].rearrange("p (j c) -> p j c", c=ROW)
        o = 2 * T + SLOT_TILES * ROW
        ys = big[:, o:o + SLOT_TILES * D].rearrange("p (j c) -> p j c", c=D)
        yg = big[:, o + SLOT_TILES * D:o + SLOT_TILES * D + T].rearrange("p (i c) -> p i c", c=D)
        h1T = big[:, 0:FB1 * T].rearrange("p (f t) -> p f t", f=FB1)
        r0 = big[:, FB1 * T:FB1 * T + 2 * TC].rearrange("p (a t) -> p a t", a=2)
        r1 = big[:, FB1 * T + 2 * TC:FB1 * T + 4 * TC].rearrange("p (a t) -> p a t", a=2)
        weff = wgu[:, 0:TOPK * F1].rearrange("p (k f) -> p k f", k=TOPK)
        eq = sb("eq", [P, TILES, E])
        wv = sb("wv", [P, TILES, E])
        lmax = sb("lmax", [P, TILES])
        fmx = sb("fmx", [P, TILES])
        oh = sb("oh", [P, TILES, E], BF16)
        th = sb("th", [P, TILES])
        score = sb("score", [P, TILES])
        cmp8 = sb("cmp8", [P, E, 8])
        nt = sb("nt", [P, E])
        nt8 = sb("nt8", [P, E, 8])
        base = sb("base", [P, E])
        endt = sb("endt", [P, E])
        sl = sb("sl", [P, TILES, E])
        slo = sb("slo", [P, TILES, E])
        slotf = sb("slotf", [P, TILES])
        slot = sb("slot", [P, TILES], U32)
        tej = sb("tej", [1, SLOT_TILES, E])
        tef = sb("tef", [1, SLOT_TILES])
        teo = sb("teo", [1, SLOT_TILES], I32)
        xs = Pe[:, :, :].rearrange("p a b -> p (a b)")[:, 0:TILES * ROW].rearrange("p (i c) -> p i c", c=ROW)
        tnh, gac = Sa, Sx
        xsT = sb("xsT", [P, 2, P])
        o = o + SLOT_TILES * D + T
        hr = big[:, o:o + 2 * F].rearrange("p (a f) -> p a f", a=2)
        hrT = big[:, o + 2 * F:o + 4 * F].rearrange("p (a f) -> p a f", a=2)

        ident = cst[:, ID:ID + P]
        onesx = cst[:, ONESX:ONESX + 64].rearrange("p (a c) -> p a c", a=2)
        tri, ones_bf = cstb[:, 0:P], cstb[:, P:2 * P]

        d_ctx, d_att0, d_att1, d_x, d_cst, d_row = map(sem, ("d_ctx", "d_att0", "d_att1", "d_x", "d_cst", "d_row"))
        d_sh, d_rgu, d_rdn, d_f1, d_bm, d_top, d_lora = map(
            sem, ("d_sh", "d_rgu", "d_rdn", "d_f1", "d_bm", "d_top", "d_lora"))
        d_tok, d_init, d_kx, d_scat, d_xs, d_yscat, d_yg, d_out = map(
            sem, ("d_tok", "d_init", "d_kx", "d_scat", "d_xs", "d_yscat", "d_yg", "d_out"))
        s_zk, s_zv, s_nh = sem("s_zk"), sem("s_zv"), sem("s_nh")
        v_chain, a_chain, g_chain = sem("v_chain"), sem("a_chain"), sem("g_chain")
        s_tg, s_bvb, s_ob, s_bo, s_xb = map(sem, ("s_tg", "s_bvb", "s_ob", "s_bo", "s_xb"))
        s_kp, s_kt, s_vp, s_ve, s_qp, s_qt = map(sem, ("s_kp", "s_kt", "s_vp", "s_ve", "s_qp", "s_qt"))
        s_ve_, s_pow, s_nmr, s_xnv, s_xna, s_xT, s_xnT = map(
            sem, ("s_var", "s_pow", "s_nmr", "s_xnv", "s_xna", "s_xT", "s_xnT"))
        s_S, s_add, s_mx, s_sub, s_exp, s_T, s_pt, s_av, s_oT, s_op, s_res = map(
            sem, ("s_S", "s_add", "s_mx", "s_sub", "s_exp", "s_T", "s_pt", "s_av", "s_oT", "s_op", "s_res"))
        s_bm = sem("s_bm")
        s_lg, s_lmax, s_th, s_oh, s_pre, s_slot, s_te, s_xs = map(
            sem, ("s_lg", "s_lmax", "s_th", "s_oh", "s_pre", "s_slot", "s_te", "s_xs"))
        s_shp, s_sht, s_shh, s_sdn, s_shr = map(sem, ("s_shp", "s_sht", "s_shh", "s_sdn", "s_shr"))
        s_t1, s_xsT, s_gu, s_rt, s_rh, s_t2, s_hT, s_y, s_ys = map(
            sem, ("s_t1", "s_xsT", "s_gu", "s_rt", "s_rh", "s_t2", "s_hT", "s_y", "s_ys"))
        s_wl, s_we, s_z, s_r1, s_h1, s_dn, s_fin = map(
            sem, ("s_wl", "s_we", "s_z", "s_r1", "s_h1", "s_dn", "s_fin"))
        XT_BANK = [(5, 6), (6, 7), (0, 1), (6, 7)]
        V_BANK, Q_BANK = [(2, 3), (5, 0)], [(7, 0), (2, 3)]
        SH_BANKS = [(3, 4), (5, 6), (7, 3), (4, 5)]
        block = ctx.enter_context(nc.Block())

        def tiles(c):
            return slice(c * TPC, (c + 1) * TPC)

        def cols(c, n=TC):
            return slice(c * n, (c + 1) * n)

        def bank3(i, n):
            return bank[i][:, 0:n * (512 // n)].rearrange("p (a b) -> p a b", a=n)

        @block.sync
        def _(sp):
            sp.dma_start(ctxT[:, :], ctx_in).then_inc(d_ctx, 16)
            sp.dma_start(xr[0][:, :, :], x_in.rearrange("(i p) d -> p i d", p=P)).then_inc(d_x, 16)
            sp.dma_start(row[:, :], bass.AP(rows.tensor, rows.offset, [[0, P], [1, ROW_COLS]])).then_inc(d_row, 16)
            sp.dma_start(tki[:, :], topi).then_inc(d_top, 16)
            sp.wait_ge(s_zk, 2)
            for c in range(CH):
                sp.wait_ge(s_kt, c + 1)
                for h in range(H):
                    r = slice(h * DK, (h + 1) * DK)
                    sp.dma_start(Kx[r, h, cols(c)], KT[r, cols(c)]).then_inc(d_kx, 16)
            sp.dma_start(xs_dram, slot_init).then_inc(d_init, 16)
            sp.dma_start(wsh[:, :], shared).then_inc(d_sh, 16)
            sp.dma_start(wgu[:, :], rgu).then_inc(d_rgu, 16)
            sp.dma_start(wdn[:, :], rdn).then_inc(d_rdn, 16)
            sp.dma_start(wat[1][:, :], att1).then_inc(d_att1, 16)
            for r in range(2):
                sp.dma_start(bia[S * r:S * r + S, :], bias).then_inc(d_bm, 16)
                m = mask[r:r + 1, :]
                sp.dma_start(msk[S * r:S * r + S, :, :],
                             bass.AP(m.tensor, m.offset, [[0, S], [2 * S, PAIRS], [1, S]])).then_inc(d_bm, 16)
            sp.dma_start(wf1[:, :], ffn1).then_inc(d_f1, 16)
            sp.wait_ge(s_T, UNITS)
            sp.dma_start(xs[:, :, D:ROW].bitcast(U32), tok_ids.rearrange("p (i c) -> p i c", c=4)).then_inc(d_tok, 16)
            sp.wait_ge(d_top, 16)
            sp.wait_ge(s_S, UNITS)
            for k in range(TOPK):
                i = sp.value_load(tki[0:1, k:k + 1], min_val=0, max_val=E - 1)
                sp.dma_start(lor[32 * k:32 * k + RANK, :], lora[bass.ds(i, 1), :, :].rearrange("a r n -> (a r) n"))\
                    .then_inc(d_lora, 16)
            sp.wait_ge(d_scat, 16 * TILES)
            for n in range(5):
                sp.dma_start(XS[:, 3 * n:3 * n + 3, :],
                             xs_dram[3 * n * P:(3 * n + 3) * P, :].rearrange("(j p) c -> p j c", p=P))\
                    .then_inc(d_xs, 16)
            sp.wait_ge(s_S, UNITS)
            for c in range(CH):
                sp.wait_ge(s_kt, CH + c + 1)
                for h in range(H):
                    r = slice(h * DK, (h + 1) * DK)
                    sp.dma_start(Kx[r, h, cols(c)], KT[r, cols(c)]).then_inc(d_kx, 16)
            sp.wait_ge(d_yscat, 16 * SLOT_TILES)
            sp.dma_start(yg, y_dram.rearrange("(i p) d -> p i d", p=P)).then_inc(d_yg, 16)
            for c in range(CH):
                sp.wait_ge(s_fin, c + 1)
                sp.dma_start(out.rearrange("(i p) d -> p i d", p=P)[:, tiles(c), :], xres[4][:, tiles(c), :])\
                    .then_inc(d_out, 16)
            sp.wait_ge(d_out, 16 * CH)

        @block.gpsimd
        def _(pool):
            links = [0]

            def link(ins):
                links[0] += 1
                ins.then_inc(g_chain, 1)
                pool.wait_ge(g_chain, links[0])

            pool.memset(Kx[:, H // 2:H, :], 0.0).then_inc(s_zk, 1)
            pool.memset(Vx[:, :, :, :], 0.0).then_inc(s_zv, 1)
            pool.memset(nhalf[:, :], -0.5).then_inc(s_nh, 1)
            pool.wait_ge(s_nh, 1)

            def rstd_of(q, c):
                pool.wait_ge(s_ve_, CH * q + c + 1)
                pool.tensor_tensor(rstd[:, tiles(c)], ve[:, tiles(c)], nhalf[:, tiles(c)], ALU.pow).then_inc(s_pow, 1)

            def residual_base(layer, c):
                pool.wait_ge(s_bo, layer + 1)
                if c == 0 and layer == 0:
                    pool.wait_ge(d_x, 16)
                if layer == 1:
                    pool.wait_ge(s_res, CH + c + 1)
                pool.tensor_tensor(xb[:, tiles(c), :], xres[2 * layer][:, tiles(c), :],
                                   mid_bcast(bo[:, :], TPC), ALU.add).then_inc(s_xb, 1)

            for c in range(CH):
                rstd_of(0, c)
            for c in range(CH):
                residual_base(0, c)
            for c in range(CH):
                rstd_of(1, c)
            pool.wait_ge(d_init, 16)
            pool.wait_ge(d_tok, 16)
            pool.wait_ge(s_slot, 1)
            pool.wait_ge(s_xs, 1)
            for i in range(TILES):
                pool.indirect_dma_start(out=xs_dram, out_offset=bass.IndirectOffsetOnAxis(ap=slot[:, i:i + 1], axis=0),
                                        in_=xs[:, i, :], in_offset=None).then_inc(d_scat, 16)
            for j in range(SLOT_TILES):
                pool.wait_ge(s_ys, j + 1)
                pool.indirect_dma_start(out=y_dram,
                                        out_offset=bass.IndirectOffsetOnAxis(ap=XS.bitcast(U32)[:, j, D:D + 1], axis=0),
                                        in_=ys[:, j, :], in_offset=None,
                                        bounds_check=T - 1, oob_is_err=False).then_inc(d_yscat, 16)
            for c in range(CH):
                rstd_of(2, c)
            for u in range(UNITS):
                U = UNITS + u
                pool.wait_ge(s_mx, u + 1)
                pool.wait_ge(s_exp, U - 1)
                pool.tensor_tensor(Sx[:, u % 2, :].rearrange("p (h k) -> p h k", h=HH),
                                   Sa[:, u % 2, :].rearrange("p (h k) -> p h k", h=HH),
                                   last_bcast(mx[:, u % 4, :], S), ALU.subtract).then_inc(s_sub, 1)
                if u in (2, 4):
                    residual_base(1, u // 2 - 1)
            for c in range(CH):
                rstd_of(3, c)

        @block.scalar
        def _(act):
            act.dma_start(wat[0][:, :], att0).then_inc(d_att0, 16)
            act.dma_start(cst[:, :], consts).then_inc(d_cst, 16)
            act.dma_start(cstb[:, :].bitcast(mybir.dt.uint16), constb).then_inc(d_cst, 16)
            act.wait_ge(d_row, 16)
            act.activation(tg[:, :], row[:, GATES:GATES + 4], ACT.Tanh).then_inc(s_tg, 1)

            def k_evac(layer):
                for c in range(CH):
                    act.wait_ge(s_kp, CH * layer + c + 1)
                    if layer == 1 and c == 0:
                        act.wait_ge(d_kx, 16 * CH * H)
                    act.activation(KT[:, cols(c)], bank[(0, 3)[layer] + c][:, :], ACT.Identity,
                                   bias=wat[layer][:, BK:BK + 1]).then_inc(s_kt, 1)

            def normalise(q, c):
                act.wait_ge(s_nmr, CH * q + c + 1)
                for i in range(c * TPC + 2, c * TPC + 4):
                    ins = act.activation(xn[:, i, :], xres[q][:, i, :], ACT.Identity,
                                         bias=nmr[:, i:i + 1], scale=rstd[:, i:i + 1])
                ins.then_inc(s_xna, 1)

            def xnT_evac(q, c):
                act.wait_ge(s_xT, CH * q + c + 1)
                act.activation(xnT[:, cols(c)], bank[XT_BANK[q][c]][:, :], ACT.Copy).then_inc(s_xnT, 1)

            def attention(layer):
                for u in range(UNITS + 1):
                    U = UNITS * layer + u
                    if u < UNITS:
                        act.wait_ge(s_sub, U + 1)
                        if U >= 3:
                            act.wait_ge(s_T, U - 2)
                        act.activation(Pe[:, u % 3, :], Sx[:, u % 2, :], ACT.Exp).then_inc(s_exp, 1)
                    if u >= 1:
                        w = u - 1
                        act.wait_ge(s_T, U)
                        act.activation(PT[:, 4 * (w % 2):4 * (w % 2) + 4, cols(w // 2, P)],
                                       bank3(2 + w % 2, 4), ACT.Copy).then_inc(s_pt, 1)

            k_evac(0)
            act.wait_ge(d_x, 16)
            for c in range(CH):
                normalise(0, c)
            for c in range(CH):
                xnT_evac(0, c)
            attention(0)
            for c in range(CH):
                normalise(1, c)
                xnT_evac(1, c)
            act.wait_ge(s_lmax, 1)
            act.activation(th[:, :], lmax[:, :], ACT.Tanh, scale=0.5).then_inc(s_th, 1)
            for n in range(4):
                act.wait_ge(s_shp, n + 1)
                if n >= 2:
                    act.wait_ge(s_shh, n - 1)
                act.activation(tnh[:, n % 2, :], bank[SH_BANKS[n][0]][:, :], ACT.Tanh, scale=0.5).then_inc(s_sht, 1)
            k_evac(1)
            for j in range(SLOT_TILES + 2):
                if j < SLOT_TILES:
                    act.wait_ge(s_t1, j + 1)
                    if j >= 2:
                        act.wait_ge(s_gu, j - 1)
                    act.activation(xsT[:, j % 2, :], bank[j % 2][:, 0:P], ACT.Copy).then_inc(s_xsT, 1)
                if 1 <= j <= SLOT_TILES:
                    w = j - 1
                    act.wait_ge(s_gu, w + 1)
                    act.wait_ge(s_shh, 4)
                    if w >= 2:
                        act.wait_ge(s_rh, w - 1)
                    act.activation(tnh[:, w % 2, 0:F], bank[2 + w % 2][:, 0:F], ACT.Tanh, scale=0.5).then_inc(s_rt, 1)
                if j >= 2:
                    w = j - 2
                    act.wait_ge(s_t2, w + 1)
                    if w >= 2:
                        act.wait_ge(s_y, w - 1)
                    act.activation(hrT[:, w % 2, :], bank[4 + w % 2][:, 0:F], ACT.Copy).then_inc(s_hT, 1)
            for c in range(CH):
                normalise(2, c)
                xnT_evac(2, c)
            attention(1)
            for c in range(CH):
                normalise(3, c)
                xnT_evac(3, c)
            for s in range(CH * FB1):
                act.wait_ge(s_z, s + 1)
                if s >= 2:
                    act.wait_ge(s_h1, s - 1)
                act.activation(r1[:, s % 2, :], bank[2 * (s % 3) + 1][:, :], ACT.Relu).then_inc(s_r1, 1)

        @block.vector
        def _(dve):
            links = [0]

            def link(ins):
                links[0] += 1
                ins.then_inc(v_chain, 1)
                dve.wait_ge(v_chain, links[0])

            def stats(q, c):
                for i in range(c * TPC, (c + 1) * TPC):
                    ins = dve.bn_stats(st[:, i, :], xres[q][:, i, :])
                link(ins)
                for i in range(c * TPC, (c + 1) * TPC):
                    ins = dve.bn_aggr(mv[:, i, :], st[:, i, :])
                link(ins)
                dve.tensor_scalar(ve[:, tiles(c)], mv[:, tiles(c), 1], EPS, None, ALU.add).then_inc(s_ve_, 1)

            def normalise(q, c):
                n = CH * q + c + 1
                dve.wait_ge(s_pow, n)
                dve.scalar_tensor_tensor(out=nmr[:, tiles(c)], in0=mv[:, tiles(c), 0], scalar=-1.0,
                                         in1=rstd[:, tiles(c)], op0=ALU.mult, op1=ALU.mult).then_inc(s_nmr, 1)
                for i in range(c * TPC, c * TPC + 2):
                    ins = dve.tensor_scalar(xn[:, i, :], xres[q][:, i, :], mv[:, i, 0:1], rstd[:, i:i + 1],
                                            ALU.subtract, ALU.mult)
                ins.then_inc(s_xnv, 1)

            def bias_cols(layer):
                dve.tensor_scalar(bvb[:, :], ident, 0.0, wat[layer][:, BV:BV + 1], ALU.mult, ALU.add).then_inc(s_bvb, 1)

            def bias_out(layer):
                dve.wait_ge(s_ob, layer + 1)
                link(dve.tensor_tensor(bo[:, :], bank[(4, 2)[layer]][:, 0:D], row[:, (BO0, BO1)[layer]:(BO0, BO1)[layer] + D],
                                       ALU.add))
                dve.tensor_scalar(bo[:, :], bo[:, :], tg[:, layer:layer + 1], None, ALU.mult).then_inc(s_bo, 1)

            def v_evac(layer):
                for c in range(CH):
                    dve.wait_ge(s_vp, CH * layer + c + 1)
                    src = bank[V_BANK[layer][c]][:, :].rearrange("p (b a e d) -> p b a e d", b=HH, a=4, e=2)
                    for r in range(2):
                        for e in range(2):
                            o = (2 * e + r) * DK
                            ins = dve.tensor_copy(
                                Vx[S * r:S * r + S, c * HH:(c + 1) * HH, e::2, o:o + DK], src[S * r:S * r + S, :, :, e, :])
                    ins.then_inc(s_ve, 1)

            def q_evac(layer):
                for c in range(CH):
                    dve.wait_ge(s_qp, CH * layer + c + 1)
                    dve.tensor_scalar(QT[:, cols(c)], bank[Q_BANK[layer][c]][:, :], wat[layer][:, BQ:BQ + 1], SCALE,
                                      ALU.add, ALU.mult).then_inc(s_qt, 1)

            def unit(layer, u):
                U = UNITS * layer + u
                ps = bank3(u % 2, HH)
                dve.wait_ge(s_S, U + 1)
                if layer == 0:
                    link(dve.tensor_reduce(mx[:, u % 4, :], ps, AX.X, ALU.max))
                    if u >= 2:
                        dve.wait_ge(s_exp, U - 1)
                    dve.tensor_tensor(Sx[:, u % 2, :].rearrange("p (h k) -> p h k", h=HH), ps,
                                      last_bcast(mx[:, u % 4, :], S), ALU.subtract).then_inc(s_sub, 1)
                else:
                    sa = Sa[:, u % 2, :].rearrange("p (h k) -> p h k", h=HH)
                    if u >= 2:
                        dve.wait_ge(s_sub, U - 1)
                    dve.tensor_tensor(sa, ps, mid_bcast(bm[:, u // 2, :], HH), ALU.add).then_inc(s_add, 1)
                    dve.wait_ge(s_add, u + 1)
                    dve.tensor_reduce(mx[:, u % 4, :], sa, AX.X, ALU.max).then_inc(s_mx, 1)

            def norm(layer, c):
                n = CH * layer + c + 1
                dve.wait_ge(s_av, n)
                link(dve.reciprocal(oT[:, cols(c)], bank[6 + c][:, :]))
                dve.tensor_tensor(oT[:, cols(c)], bank[4 + c][:, :], oT[:, cols(c)], ALU.mult).then_inc(s_oT, 1)

            def residual(layer, c):
                n = CH * layer + c + 1
                dve.wait_ge(s_op, n)
                dve.wait_ge(s_xb, n)
                dve.scalar_tensor_tensor(out=xres[2 * layer + 1][:, tiles(c), :], in0=bank3(4 + c, TPC),
                                         scalar=tg[:, layer:layer + 1], in1=xb[:, tiles(c), :],
                                         op0=ALU.mult, op1=ALU.add).then_inc(s_res, 1)
                dve.wait_ge(s_res, CH * 2 * layer + c + 1)

            def attention(layer):
                for u in range(UNITS):
                    unit(layer, u)
                    if u == UNITS - 4:
                        norm(layer, 0)
                residual(layer, 0)
                stats(2 * layer + 1, 0)
                norm(layer, 1)
                normalise(2 * layer + 1, 0)
                residual(layer, 1)
                stats(2 * layer + 1, 1)
                normalise(2 * layer + 1, 1)

            dve.memset(Kx[:, 0:H // 2, :], 0.0).then_inc(s_zk, 1)
            dve.wait_ge(d_cst, 32)
            dve.wait_ge(d_att0, 16)
            bias_cols(0)
            dve.wait_ge(d_x, 16)
            stats(0, 0)
            stats(0, 1)
            normalise(0, 0)
            normalise(0, 1)
            dve.wait_ge(s_zv, 1)
            v_evac(0)
            q_evac(0)
            dve.wait_ge(s_tg, 1)
            dve.wait_ge(d_row, 16)
            bias_out(0)
            attention(0)

            dve.wait_ge(s_lg, 1)
            lg = bank[0][:, 0:TILES * E].rearrange("p (i e) -> p i e", e=E)
            dve.tensor_reduce(lmax[:, :], lg, AX.X, ALU.max).then_inc(s_lmax, 1)
            dve.wait_ge(s_lmax, 1)
            link(dve.tensor_tensor(eq[:, :, :], lg, last_bcast(lmax[:, :], E), ALU.is_equal))
            link(dve.tensor_tensor(wv[:, :, :], eq[:, :, :], mid_bcast(cst[:, W8:W8 + E], TILES), ALU.mult))
            link(dve.tensor_reduce(fmx[:, :], wv[:, :, :], AX.X, ALU.max))
            dve.tensor_tensor(oh[:, :, :], wv[:, :, :], last_bcast(fmx[:, :], E), ALU.is_equal).then_inc(s_oh, 1)
            dve.wait_ge(s_th, 1)
            link(dve.tensor_scalar(score[:, :], th[:, :], 0.5, 0.5, ALU.mult, ALU.add))
            dve.tensor_tensor(xs[:, :, 0:D], xn[:, :, :], last_bcast(score[:, :], D), ALU.mult).then_inc(s_xs, 1)
            dve.wait_ge(s_pre, 1)
            link(dve.tensor_tensor(cmp8[:, :, :], last_bcast(bank[2][:, 0:E], 8), mid_bcast(cst[:, THR:THR + 8], E),
                                   ALU.is_gt))
            link(dve.tensor_reduce(nt[:, :], cmp8[:, :, :], AX.X, ALU.add))
            link(dve.tensor_tensor(nt8[:, :, :], mid_bcast(nt[:, :], E),
                                   cst[:, TRI8:TRI8 + 64].rearrange("p (a b) -> p a b", a=E), ALU.mult))
            link(dve.tensor_reduce(base[:, :], nt8[:, :, :], AX.X, ALU.add))
            link(dve.scalar_tensor_tensor(out=sl[:, :, :], in0=mid_bcast(base[:, :], TILES), scalar=float(P),
                                          in1=bank[1][:, 0:TILES * E].rearrange("p (i e) -> p i e", e=E),
                                          op0=ALU.mult, op1=ALU.add))
            link(dve.tensor_tensor(slo[:, :, :], sl[:, :, :], oh[:, :, :], ALU.mult))
            link(dve.tensor_reduce(slotf[:, :], slo[:, :, :], AX.X, ALU.add))
            dve.tensor_copy(slot[:, :], slotf[:, :]).then_inc(s_slot, 1)
            link(dve.tensor_tensor(endt[:, :], base[:, :], nt[:, :], ALU.add))
            link(dve.tensor_tensor(tej[:, :, :], mid_bcast(endt[0:1, :], SLOT_TILES),
                                   last_bcast(cst[0:1, JT:JT + SLOT_TILES], E), ALU.is_le))
            link(dve.tensor_reduce(tef[:, :], tej[:, :, :], AX.X, ALU.add))
            dve.tensor_scalar(teo[:, :], tef[:, :], float(E - 1), float(2 * D), ALU.min, ALU.mult).then_inc(s_te, 1)

            for n in range(4):
                c, f = n // 2, n % 2
                g, up = SH_BANKS[n]
                dve.wait_ge(s_sht, n + 1)
                link(dve.scalar_tensor_tensor(out=gac[:, n % 2, :], in0=tnh[:, n % 2, :], scalar=1.0,
                                              in1=bank[g][:, :], op0=ALU.add, op1=ALU.mult))
                dve.scalar_tensor_tensor(out=hsT[:, f, cols(c)], in0=gac[:, n % 2, :], scalar=0.5,
                                         in1=bank[up][:, :], op0=ALU.mult, op1=ALU.mult).then_inc(s_shh, 1)
            for c in range(CH):
                dve.wait_ge(s_sdn, c + 1)
                dve.scalar_tensor_tensor(out=xb[:, tiles(c), :], in0=bank3(6 + c, TPC), scalar=tg[:, 2:3],
                                         in1=xres[1][:, tiles(c), :], op0=ALU.mult, op1=ALU.add).then_inc(s_shr, 1)
            dve.wait_ge(d_att1, 16)
            bias_cols(1)
            v_evac(1)
            bias_out(1)
            dve.wait_ge(d_bm, 64)
            link(dve.tensor_scalar(bm[:, :, :], msk[:, :, :], NEG, None, ALU.mult))
            link(dve.tensor_tensor(bm[:, :, :], bm[:, :, :], mid_bcast(bia[:, :], PAIRS), ALU.add))
            for j in range(SLOT_TILES + 2):
                if j < SLOT_TILES:
                    g = bank[2 + j % 2]
                    dve.wait_ge(s_rt, j + 1)
                    link(dve.scalar_tensor_tensor(out=gac[:, j % 2, 0:F], in0=tnh[:, j % 2, 0:F], scalar=1.0,
                                                  in1=g[:, 0:F], op0=ALU.add, op1=ALU.mult))
                    if j >= 2:
                        dve.wait_ge(s_t2, j - 1)
                    dve.scalar_tensor_tensor(out=hr[:, j % 2, :], in0=gac[:, j % 2, 0:F], scalar=0.5,
                                             in1=g[:, F:2 * F], op0=ALU.mult, op1=ALU.mult).then_inc(s_rh, 1)
                if j >= 2:
                    w = j - 2
                    dve.wait_ge(s_y, w + 1)
                    dve.tensor_copy(ys[:, w, :], bank[6 + w % 2][:, 0:D]).then_inc(s_ys, 1)
            for k in range(TOPK):
                dve.wait_ge(s_wl, k + 1)
                if k == 0:
                    dve.wait_ge(d_f1, 16)
                dve.tensor_tensor(weff[:, k, :], bank[4 + k][:, :], wf1[:, 0:F1], ALU.add).then_inc(s_we, 1)
            dve.wait_ge(d_yg, 16)
            for c in range(CH):
                dve.scalar_tensor_tensor(out=xres[2][:, tiles(c), :], in0=yg[:, tiles(c), :], scalar=tg[:, 2:3],
                                         in1=xb[:, tiles(c), :], op0=ALU.mult, op1=ALU.add).then_inc(s_res, 1)
                dve.wait_ge(s_res, CH + c + 1)
                stats(2, c)
            for c in range(CH):
                normalise(2, c)
            q_evac(1)
            attention(1)
            for s in range(CH * FB1):
                c, f = s // FB1, s % FB1
                dve.wait_ge(s_z, s + 1)
                link(dve.tensor_scalar(r0[:, s % 2, :], bank[2 * (s % 3)][:, :], 0.0, row[:, TOPV:TOPV + 1],
                                       ALU.max, ALU.mult))
                dve.wait_ge(s_r1, s + 1)
                dve.scalar_tensor_tensor(out=h1T[:, f, cols(c)], in0=r1[:, s % 2, :], scalar=row[:, TOPV + 1:TOPV + 2],
                                         in1=r0[:, s % 2, :], op0=ALU.mult, op1=ALU.add).then_inc(s_h1, 1)
            for c in range(CH):
                dve.wait_ge(s_dn, c + 1)
                dve.scalar_tensor_tensor(out=xres[4][:, tiles(c), :], in0=bank3(6 + c, TPC), scalar=tg[:, 3:4],
                                         in1=xres[3][:, tiles(c), :], op0=ALU.mult, op1=ALU.add).then_inc(s_fin, 1)

        @block.tensor
        def _(pe):
            def mm(o, l, r, first=True, last=True, **k):
                return pe.matmul(o, l, r, start=first, stop=last, **k)

            def k_proj(layer):
                for c in range(CH):
                    mm(bank[(0, 3)[layer] + c][:, :], wat[layer][:, WK:WK + D], ctxT[:, cols(c)]).then_inc(s_kp, 1)

            def v_proj(layer):
                wvt = wat[layer][:, WV:WV + D].rearrange("p (a r d) -> p r a d", r=2, d=DK)
                for c in range(CH):
                    for n in range(HH):
                        b = c * HH + n
                        for r in range(2):
                            o = bank[V_BANK[layer][c]][S * r:S * r + S, n * S:(n + 1) * S]
                            ins = mm(o.rearrange("p (a d) -> p a d", d=DK), ctxT[:, b * S:(b + 1) * S], wvt[:, r])
                    ins.then_inc(s_vp, 1)

            def out_bias(layer):
                pe.wait_ge(s_bvb, layer + 1)
                mm(bank[(4, 2)[layer]][:, 0:D], bvb[:, :], wat[layer][:, WO:WO + D]).then_inc(s_ob, 1)

            def xn_transpose(q, c):
                n = CH * q + c + 1
                pe.wait_ge(s_xnv, n)
                pe.wait_ge(s_xna, n)
                for i in range(TPC):
                    ins = pe.transpose(bank[XT_BANK[q][c]][:, i * P:(i + 1) * P], xn[:, c * TPC + i, :], ident)
                ins.then_inc(s_xT, 1)

            def q_proj(layer):
                for c in range(CH):
                    pe.wait_ge(s_xnT, CH * 2 * layer + c + 1)
                    if layer == 0 and c == 1:
                        pe.wait_ge(s_kt, 1)
                    mm(bank[Q_BANK[layer][c]][:, :], wat[layer][:, WQ:WQ + D], xnT[:, cols(c)]).then_inc(s_qp, 1)

            def scores(layer, u):
                U = UNITS * layer + u
                bp, hh = u // 2, u % 2
                if u >= 2:
                    if layer == 0:
                        pe.wait_ge(s_sub, U - 1)
                    else:
                        pe.wait_ge(s_add, u - 1)
                for r in range(2):
                    b = 2 * bp + r
                    ins = mm(bank[u % 2][S * r:S * r + S, :].rearrange("p (h k) -> p h k", h=HH),
                             QT[:, b * S:(b + 1) * S], Kx[:, HH * hh:HH * (hh + 1), b * S:(b + 1) * S])
                ins.then_inc(s_S, 1)

            def transposes(layer, u):
                U = UNITS * layer + u
                pe.wait_ge(s_exp, U + 1)
                if U >= 2:
                    pe.wait_ge(s_pt, U - 1)
                for m in range(4):
                    ins = pe.transpose(bank[2 + u % 2][:, m * P:(m + 1) * P], Pe[:, u % 3, m * P:(m + 1) * P], ident)
                ins.then_inc(s_T, 1)

            def values(layer, bp):
                c = bp // (PAIRS // CH)
                pe.wait_ge(s_pt, UNITS * layer + 2 * bp + 2)
                local = (bp % (PAIRS // CH)) * P
                for r in range(2):
                    b = 2 * bp + r
                    for e in range(2):
                        for g in range(4):
                            a = 2 * g + e
                            mm(bank[4 + c][32 * g:32 * g + 32, local + S * r:local + S * r + S], Vx[:, b, a, :],
                               PT[:, a, b * S:(b + 1) * S], first=(e == 0), last=(e == 1), tile_position=(0, 32 * g))
                for e in range(2):
                    for g in range(4):
                        a = 2 * g + e
                        ins = mm(bank[6 + c][32 * g:32 * g + 32, local:local + P], onesx[:, e, :],
                                 PT[:, a, bp * P:(bp + 1) * P], first=(e == 0), last=(e == 1), tile_position=(0, 32 * g))
                if bp % (PAIRS // CH) == PAIRS // CH - 1:
                    ins.then_inc(s_av, 1)

            def out_proj(layer, c):
                pe.wait_ge(s_oT, CH * layer + c + 1)
                for i in range(TPC):
                    t = c * TPC + i
                    ins = mm(bank[4 + c][:, i * D:(i + 1) * D], oT[:, t * P:(t + 1) * P], wat[layer][:, WO:WO + D])
                ins.then_inc(s_op, 1)

            def attention(layer):
                pe.wait_ge(d_kx, 16 * H * CH * (layer + 1))
                for c in range(CH):
                    pe.wait_ge(s_qt, CH * layer + c + 1)
                    pe.wait_ge(s_ve, CH * layer + c + 1)
                for bp in range(PAIRS + 1):
                    for hh in range(2):
                        if bp < PAIRS:
                            scores(layer, 2 * bp + hh)
                        if bp >= 1:
                            transposes(layer, 2 * bp - 2 + hh)
                    if bp >= 2:
                        values(layer, bp - 2)
                out_proj(layer, 0)
                values(layer, PAIRS - 1)
                out_proj(layer, 1)

            pe.wait_ge(d_ctx, 16)
            pe.wait_ge(d_att0, 16)
            k_proj(0)
            v_proj(0)
            pe.wait_ge(d_cst, 32)
            for c in range(CH):
                xn_transpose(0, c)
            q_proj(0)
            out_bias(0)
            pe.wait_ge(s_bo, 1)
            attention(0)

            for c in range(CH):
                xn_transpose(1, c)
            for c in range(CH):
                pe.wait_ge(s_xnT, CH + c + 1)
                for i in range(c * TPC, (c + 1) * TPC):
                    ins = mm(bank[0][:, i * E:(i + 1) * E], xnT[:, i * P:(i + 1) * P], wat[0][:, WGATE:WGATE + E])
            ins.then_inc(s_lg, 1)

            def shared_up(n):
                c, f = n // 2, n % 2
                if n == 0:
                    pe.wait_ge(d_sh, 16)
                    pe.wait_ge(s_res, CH)
                if n >= 2:
                    pe.wait_ge(s_shh, n - 1)
                for k in range(2):
                    ins = mm(bank[SH_BANKS[n][k]][:, :], wsh[:, k * F + f * P:k * F + (f + 1) * P], xnT[:, cols(c)])
                ins.then_inc(s_shp, 1)

            shared_up(0)
            pe.wait_ge(s_oh, 1)
            mm(bank[1][:, 0:TILES * E], tri, oh[:, :, :].rearrange("p i e -> p (i e)"), skip_group_check=True)
            for s in range(1, TILES):
                mm(bank[1][:, s * E:TILES * E], ones_bf, oh[:, 0:TILES - s, :].rearrange("p i e -> p (i e)"),
                   first=False, skip_group_check=True)
            for i in range(TILES):
                ins = mm(bank[2][:, 0:E], ones_bf, oh[:, i, :], first=(i == 0), last=(i == TILES - 1))
            ins.then_inc(s_pre, 1)
            for n in range(1, 4):
                shared_up(n)
            for c in range(CH):
                pe.wait_ge(s_shh, (3, 4)[c])
                for i in range(TPC):
                    t = c * TPC + i
                    for f in range(2):
                        ins = mm(bank[6 + c][:, i * D:(i + 1) * D], hsT[:, f, t * P:(t + 1) * P],
                                 wsh[:, 2 * F + f * D:2 * F + (f + 1) * D], first=(f == 0), last=(f == 1))
                ins.then_inc(s_sdn, 1)
            pe.wait_ge(d_att1, 16)
            k_proj(1)
            pe.wait_ge(s_te, 1)
            v_proj(1)
            out_bias(1)

            pe.wait_ge(d_rgu, 16)
            pe.wait_ge(d_rdn, 16)
            pe.wait_ge(s_ve, 2 * CH)
            pe.wait_ge(s_bo, 2)
            pe.wait_ge(s_kt, 2 * CH)
            pe.wait_ge(s_shr, CH)
            first_col = {}
            for j in range(SLOT_TILES + 3):
                if j < SLOT_TILES:
                    if j % 3 == 0:
                        pe.wait_ge(d_xs, 16 * 5 if j else 16 * 5)
                    if j >= 2:
                        pe.wait_ge(s_xsT, j - 1)
                    pe.transpose(bank[j % 2][:, 0:P], XS[:, j, 0:D], ident).then_inc(s_t1, 1)
                if 1 <= j <= SLOT_TILES:
                    w = j - 1
                    e = pe.value_load(teo[0:1, w:w + 1], min_val=0, max_val=(E - 1) * 2 * D)
                    first_col[w] = e
                    pe.wait_ge(s_xsT, w + 1)
                    if w >= 2:
                        pe.wait_ge(s_rh, w - 1)
                    mm(bank[2 + w % 2][:, :], xsT[:, w % 2, :], wgu[:, bass.ds(e * 2, 2 * F)]).then_inc(s_gu, 1)
                if 2 <= j <= SLOT_TILES + 1:
                    w = j - 2
                    pe.wait_ge(s_rh, w + 1)
                    if w >= 2:
                        pe.wait_ge(s_hT, w - 1)
                    for f in range(2):
                        ins = pe.transpose(bank[4 + w % 2][:, f * P:(f + 1) * P], hr[:, w % 2, f * P:(f + 1) * P], ident)
                    ins.then_inc(s_t2, 1)
                if j >= 3:
                    w = j - 3
                    e = first_col[w]
                    pe.wait_ge(s_hT, w + 1)
                    if w >= 2:
                        pe.wait_ge(s_ys, w - 1)
                    for f in range(2):
                        ins = mm(bank[6 + w % 2][:, 0:D], hrT[:, w % 2, f * P:(f + 1) * P],
                                 wdn[:, bass.ds(e + f * D, D)], first=(f == 0), last=(f == 1))
                    ins.then_inc(s_y, 1)
            pe.wait_ge(d_lora, 32)
            pe.wait_ge(s_hT, SLOT_TILES)
            for k in range(TOPK):
                r = slice(32 * k, 32 * k + RANK)
                mm(bank[4 + k][:, :], lor[r, 0:D], lor[r, D:D + F1]).then_inc(s_wl, 1)

            for c in range(CH):
                xn_transpose(2, c)
            q_proj(1)
            attention(1)
            for c in range(CH):
                xn_transpose(3, c)
            for s in range(CH * FB1 + 1):
                if s < CH * FB1:
                    c, f = s // FB1, s % FB1
                    if f == 0:
                        pe.wait_ge(s_xnT, CH * 3 + c + 1)
                    if s == 0:
                        pe.wait_ge(s_we, TOPK)
                    if s == 2:
                        pe.wait_ge(s_res, 3 * CH)
                    if s >= 3:
                        pe.wait_ge(s_h1, s - 2)
                    for k in range(TOPK):
                        ins = mm(bank[2 * (s % 3) + k][:, :], weff[:, k, f * P:(f + 1) * P], xnT[:, cols(c)])
                    ins.then_inc(s_z, 1)
                if s >= 1 and (s - 1) % FB1 == FB1 - 1:
                    c = (s - 1) // FB1
                    pe.wait_ge(s_h1, (c + 1) * FB1)
                    for i in range(TPC):
                        t = c * TPC + i
                        for f in range(FB1):
                            ins = mm(bank[6 + c][:, i * D:(i + 1) * D], h1T[:, f, t * P:(t + 1) * P],
                                     wf1[:, F1 + f * D:F1 + (f + 1) * D], first=(f == 0), last=(f == FB1 - 1))
                    ins.then_inc(s_dn, 1)


_ORDER = ["x_in", "ctx_in", "att0", "att1", "consts", "constb", "rows", "shared", "rgu", "rdn", "ffn1", "lora",
          "topi", "bias", "mask", "tok_ids", "slot_init"]


def pack(a):
    import numpy as np

    def col(v):
        return v.reshape(-1, 1)

    wi, bi = a["L1_xattn_in_proj_w"], a["L1_xattn_in_proj_b"]
    consts = np.zeros((P, CONST_COLS), np.float32)
    consts[:, ID:ID + P] = np.eye(P)
    for p in range(P):
        for e in range(2):
            o = ONESX + 32 * e + (2 * e + p // S) * DK
            consts[p, o:o + DK] = 1.0
    consts[:, W8:W8 + E] = np.arange(E, 0, -1)
    consts[:, THR:THR + 8] = np.arange(8) * P
    consts[:, TRI8:TRI8 + 64] = np.tril(np.ones((E, E)), -1).reshape(-1)
    consts[:, JT:JT + 16] = np.arange(16)
    one = 0x3F80
    constb = np.full((P, 2 * P), one, np.uint16)
    constb[:, 0:P] = np.triu(np.ones((P, P)), 1).astype(np.uint16) * one
    tok = np.zeros((P, TILES, 4), np.uint32)
    tok[:, :, 0] = np.arange(TILES)[None, :] * P + np.arange(P)[:, None]
    init = np.zeros((SLOT_TILES * P, ROW), np.uint32)
    init[:, D] = 4 * T + np.arange(SLOT_TILES * P)
    pad = np.zeros((D, E), np.float32)
    return {
        "x_in": a["x"].reshape(T, D),
        "ctx_in": a["ctx_1024"].reshape(T, D).T,
        "att0": np.concatenate([a["L0_xattn_Wk"].T, a["L0_xattn_Wv"].T, col(a["L0_xattn_bk"]), col(a["L0_xattn_bv"]),
                                col(a["L0_xattn_bq"]), a["L0_xattn_Wq"].T, a["L0_xattn_Wo"].T,
                                a["L0_ffn_gate_w"].T], 1),
        "att1": np.concatenate([wi[D:2 * D].T, wi[2 * D:].T, col(bi[D:2 * D]), col(bi[2 * D:]), col(bi[:D]),
                                wi[:D].T, a["L1_xattn_out_proj_w"].T, pad], 1),
        "consts": consts,
        "constb": constb,
        "rows": np.concatenate([a["L0_xattn_bo"], a["L1_xattn_out_proj_b"], a["g_xattn"], a["g_ffn"],
                                a["L1_ffn_top_k_values"]]).reshape(1, -1),
        "shared": np.concatenate([a["L0_ffn_shared_gate"].T, a["L0_ffn_shared_up"].T,
                                  a["L0_ffn_shared_down"].T.reshape(2, P, D).transpose(1, 0, 2).reshape(P, 2 * D)], 1),
        "rgu": np.stack([a["L0_ffn_r_gate"].transpose(2, 0, 1), a["L0_ffn_r_up"].transpose(2, 0, 1)], 2)
                 .reshape(D, E * 2 * F),
        "rdn": a["L0_ffn_r_down"].transpose(2, 0, 1).reshape(2, P, E, D).transpose(1, 2, 0, 3).reshape(P, E * 2 * D),
        "ffn1": np.concatenate([a["L1_ffn_wi_w"].T,
                                a["L1_ffn_wo_w"].T.reshape(FB1, P, D).transpose(1, 0, 2).reshape(P, F1)], 1),
        "lora": np.concatenate([a["L1_ffn_lora_As"], a["L1_ffn_lora_Bs"].transpose(0, 2, 1)], 2),
        "topi": a["L1_ffn_top_k_indices"].reshape(1, TOPK),
        "bias": a["fside_1xSxS2_0"][0],
        "mask": a["mask_BxS2_bk0"],
        "tok_ids": tok.reshape(P, TILES * 4),
        "slot_init": init.view(np.float32),
    }


def kernel(**inputs):
    import numpy as _np
    import concourse.bacc as _bacc
    from concourse import mybir as _mybir
    from concourse.bass_utils import run_bass_kernel_spmd as _run

    nc = _bacc.Bacc("TRN2", target_bir_lowering=False, num_devices=1)
    packed = pack({k: _np.asarray(v) for k, v in inputs.items()})
    arrays, args = {}, []
    for name in _ORDER:
        a = _np.ascontiguousarray(packed[name])
        arrays[name] = a
        args.append(nc.dram_tensor(name, a.shape, _mybir.dt.from_np(a.dtype), kind="ExternalInput").ap())
    out = nc.dram_tensor("out", (T, D), F32, kind="ExternalOutput").ap()
    build(nc, *args, out)
    r = _run(nc, [arrays], core_ids=[0])
    return r.results[0]["out"].reshape(B, S, D)
```

```python
from contextlib import ExitStack

import concourse.bass as bass
from concourse import mybir

F32 = mybir.dt.float32
BF16 = mybir.dt.bfloat16
U32 = mybir.dt.uint32
I32 = mybir.dt.int32
ALU = mybir.AluOpType
ACT = mybir.ActivationFunctionType
AX = mybir.AxisListType

B, S, D = 16, 64, 128
H, DK = 16, 8
T = B * S
P = 128
TILES = T // P
CH = 2
TPC = TILES // CH
TC = T // CH
PIECES = 4
TPP = TILES // PIECES
PAIRS = B // 2
UNITS = PAIRS * 2
HH = H // 2
HP = H // 2
E, F = 8, 256
SLOT_TILES = TILES + E - 1
ROW = D + 4
F1 = 512
FB1 = F1 // P
RANK, TOPK = 16, 2
SCALE = DK ** -0.5
EPS = 1e-5
NEG = -3.4028234663852886e38

WK, WV, BK, BV, BQ = 0, D, 2 * D, 2 * D + 1, 2 * D + 2
WQ, WO, WGATE = 2 * D + 3, 3 * D + 3, 4 * D + 3
ATT_COLS = 4 * D + 3 + E
ID, ONESX, W8, THR, TRI8, JT = 0, 128, 192, 200, 208, 272
HM = JT + 16
CONST_COLS = HM + H
BO0, BO1, GATES, TOPV = 0, D, 2 * D, 2 * D + 4
ROW_COLS = 2 * D + 4 + TOPK


def last_bcast(ap, n):
    return bass.AP(ap.tensor, ap.offset, [list(d) for d in ap.ap] + [[0, n]])


def mid_bcast(ap, n):
    dims = [list(d) for d in ap.ap]
    return bass.AP(ap.tensor, ap.offset, dims[:1] + [[0, n]] + dims[1:])


def build(nc, x_in, ctx_in, att0, att1, consts, constb, rows, shared, rgu, rdn, ffn1, lora, topi,
          bias, mask, tok_ids, slot_init, out):
    with ExitStack() as ctx:
        def sb(name, shape, dt=F32):
            return ctx.enter_context(nc.sbuf_tensor(name, shape, dt))

        def sem(name):
            return ctx.enter_context(nc.semaphore(name))

        bank = [ctx.enter_context(nc.psum_tensor(f"bank{i}", [P, 512], F32)) for i in range(8)]
        xs_dram = nc.dram_tensor("sorted_rows", [SLOT_TILES * P, ROW], F32).ap()
        y_dram = nc.dram_tensor("routed_rows", [T, D], F32).ap()

        ctxT = sb("ctxT", [P, T])
        wat = [sb("wat0", [P, ATT_COLS]), sb("wat1", [P, ATT_COLS])]
        cst = sb("cst", [P, CONST_COLS])
        cstb = sb("cstb", [P, 2 * P], BF16)
        row = sb("row", [P, ROW_COLS])
        wsh = sb("wsh", [P, 3 * F])
        wgu = sb("wgu", [P, E * 2 * F])
        wdn = sb("wdn", [P, E * 2 * D])
        wf1 = sb("wf1", [P, 2 * F1])
        tki = sb("tki", [1, TOPK], I32)
        msk = sb("msk", [P, PAIRS, S], mybir.dt.uint8)
        bia = sb("bia", [P, S])
        bm = wsh[:, 0:PAIRS * S].rearrange("p (a k) -> p a k", a=PAIRS)
        tg = sb("tg", [P, 4])
        xr = [sb(f"xr{i}", [P, TILES, D]) for i in range(2)]
        xres = [xr[0], xr[1], xr[0], xr[1], xr[0]]
        xb = sb("xb", [P, TILES, D])
        xn = sb("xn", [P, TILES, D])
        xnT = sb("xnT", [P, T])
        st = sb("st", [P, TILES, 6])
        mv = sb("mv", [P, TILES, 2])
        ve = sb("ve", [P, TILES])
        nhalf = sb("nhalf", [P, TILES])
        rstd = sb("rstd", [P, TILES])
        nmr = sb("nmr", [P, TILES])
        KT = sb("KT", [P, T])
        QT = sb("QT", [P, T])
        lor = QT[:, 0:D + F1]
        oT = sb("oT", [P, T])
        Kx = sb("Kx", [P, H, T])
        Vx = sb("Vx", [P, B, HP, 32])
        Sa = sb("Sa", [P, 2, HH * S])
        Sx = sb("Sx", [P, 2, HH * S])
        Pe = sb("Pe", [P, 3, HH * S])
        mx = sb("mx", [P, 4, HH])
        bvb = sb("bvb", [P, D])
        bo = sb("bo", [P, D])
        big = sb("big", [P, HP * T])
        PT = big[:, :].rearrange("p (a t) -> p a t", a=HP)
        hsT = big[:, 0:2 * T].rearrange("p (f t) -> p f t", f=2)
        XS = big[:, 2 * T:2 * T + SLOT_TILES * ROW].rearrange("p (j c) -> p j c", c=ROW)
        o = 2 * T + SLOT_TILES * ROW
        ys = big[:, o:o + SLOT_TILES * D].rearrange("p (j c) -> p j c", c=D)
        yg = big[:, o + SLOT_TILES * D:o + SLOT_TILES * D + T].rearrange("p (i c) -> p i c", c=D)
        h1T = big[:, 0:FB1 * T].rearrange("p (f t) -> p f t", f=FB1)
        r0 = big[:, FB1 * T:FB1 * T + 2 * TC].rearrange("p (a t) -> p a t", a=2)
        r1 = big[:, FB1 * T + 2 * TC:FB1 * T + 4 * TC].rearrange("p (a t) -> p a t", a=2)
        weff = wgu[:, 0:TOPK * F1].rearrange("p (k f) -> p k f", k=TOPK)
        eq = sb("eq", [P, TILES, E])
        wv = sb("wv", [P, TILES, E])
        lmax = sb("lmax", [P, TILES])
        fmx = sb("fmx", [P, TILES])
        oh = sb("oh", [P, TILES, E], BF16)
        th = sb("th", [P, TILES])
        score = sb("score", [P, TILES])
        cmp8 = sb("cmp8", [P, E, 8])
        nt = sb("nt", [P, E])
        nt8 = sb("nt8", [P, E, 8])
        base = sb("base", [P, E])
        endt = sb("endt", [P, E])
        sl = sb("sl", [P, TILES, E])
        slo = sb("slo", [P, TILES, E])
        slotf = sb("slotf", [P, TILES])
        slot = sb("slot", [P, TILES], U32)
        tej = sb("tej", [1, SLOT_TILES, E])
        tef = sb("tef", [1, SLOT_TILES])
        teo = sb("teo", [1, SLOT_TILES], I32)
        xs = Pe[:, :, :].rearrange("p a b -> p (a b)")[:, 0:TILES * ROW].rearrange("p (i c) -> p i c", c=ROW)
        tnh, gac = Sa, Sx
        xsT = sb("xsT", [P, 2, P])
        o = o + SLOT_TILES * D + T
        hr = big[:, o:o + 2 * F].rearrange("p (a f) -> p a f", a=2)
        hrT = big[:, o + 2 * F:o + 4 * F].rearrange("p (a f) -> p a f", a=2)

        ident = cst[:, ID:ID + P]
        onesx = cst[:, ONESX:ONESX + 64].rearrange("p (a c) -> p a c", a=2)
        tri, ones_bf = cstb[:, 0:P], cstb[:, P:2 * P]

        d_ctx, d_att0, d_att1, d_x, d_cst, d_row = map(sem, ("d_ctx", "d_att0", "d_att1", "d_x", "d_cst", "d_row"))
        d_sh, d_rgu, d_rdn, d_f1, d_bm, d_top, d_lora = map(
            sem, ("d_sh", "d_rgu", "d_rdn", "d_f1", "d_bm", "d_top", "d_lora"))
        d_tok, d_init, d_kx, d_scat, d_xs, d_yscat, d_yg, d_out = map(
            sem, ("d_tok", "d_init", "d_kx", "d_scat", "d_xs", "d_yscat", "d_yg", "d_out"))
        s_zv, s_nh, s_kx0, s_kx1, s_kxa = map(sem, ("s_zv", "s_nh", "s_kx0", "s_kx1", "s_kxa"))
        v_chain, a_chain, g_chain = sem("v_chain"), sem("a_chain"), sem("g_chain")
        s_tg, s_bvb, s_ob, s_bo, s_xb = map(sem, ("s_tg", "s_bvb", "s_ob", "s_bo", "s_xb"))
        s_kp, s_kt, s_vp, s_ve, s_qp, s_qt = map(sem, ("s_kp", "s_kt", "s_vp", "s_ve", "s_qp", "s_qt"))
        s_ve_, s_pow, s_nmr, s_xnv, s_xna, s_xT, s_xnT = map(
            sem, ("s_var", "s_pow", "s_nmr", "s_xnv", "s_xna", "s_xT", "s_xnT"))
        s_S, s_add, s_mx, s_sub, s_exp, s_T, s_pt, s_av, s_oT, s_op, s_res = map(
            sem, ("s_S", "s_add", "s_mx", "s_sub", "s_exp", "s_T", "s_pt", "s_av", "s_oT", "s_op", "s_res"))
        s_bm = sem("s_bm")
        s_lg, s_lmax, s_th, s_oh, s_pre, s_slot, s_te, s_xs = map(
            sem, ("s_lg", "s_lmax", "s_th", "s_oh", "s_pre", "s_slot", "s_te", "s_xs"))
        s_shp, s_sht, s_shh, s_sdn, s_shr = map(sem, ("s_shp", "s_sht", "s_shh", "s_sdn", "s_shr"))
        s_t1, s_xsT, s_gu, s_rt, s_rh, s_t2, s_hT, s_y, s_ys = map(
            sem, ("s_t1", "s_xsT", "s_gu", "s_rt", "s_rh", "s_t2", "s_hT", "s_y", "s_ys"))
        s_wl, s_we, s_z, s_r1, s_h1, s_dn, s_fin = map(
            sem, ("s_wl", "s_we", "s_z", "s_r1", "s_h1", "s_dn", "s_fin"))
        XT_BANK = [(4, 5, 6, 7), (7,) * 4, (0, 1, 4, 5), (7,) * 4]
        V_BANK, Q_BANK = [(2, 3), (5, 0)], [(0, 1), (2, 3)]
        OB_BANK = (2, 2)
        SH_BANKS = [(0, 1), (2, 3), (5, 6), (7, 0)]
        ACT_HEADS = 6
        RES_X2, RES_L1 = PIECES, PIECES + CH
        block = ctx.enter_context(nc.Block())

        def tiles(c):
            return slice(c * TPC, (c + 1) * TPC)

        def cols(c, n=TC):
            return slice(c * n, (c + 1) * n)

        def piece(a):
            return slice(a * TPP, (a + 1) * TPP)

        def stat_count(q, a):
            return (0, 2, 6, 8)[q] + (a // 2 if q % 2 == 0 else a) + 1

        def bank3(i, n):
            return bank[i][:, 0:n * (512 // n)].rearrange("p (a b) -> p a b", a=n)

        @block.sync
        def _(sp):
            for c in range(CH):
                sp.dma_start(xr[0][:, tiles(c), :], x_in.rearrange("(i p) d -> p i d", p=P)[:, tiles(c), :])\
                    .then_inc(d_x, 16)
            sp.dma_start(ctxT[:, :], ctx_in).then_inc(d_ctx, 16)
            sp.dma_start(row[:, :], bass.AP(rows.tensor, rows.offset, [[0, P], [1, ROW_COLS]])).then_inc(d_row, 16)
            sp.dma_start(tki[:, :], topi).then_inc(d_top, 16)
            sp.dma_start(xs_dram, slot_init).then_inc(d_init, 16)
            sp.dma_start(wsh[:, :], shared).then_inc(d_sh, 16)
            sp.dma_start(wgu[:, :], rgu).then_inc(d_rgu, 16)
            sp.dma_start(wdn[:, :], rdn).then_inc(d_rdn, 16)
            sp.dma_start(wat[1][:, :], att1).then_inc(d_att1, 16)
            for r in range(2):
                sp.dma_start(bia[S * r:S * r + S, :], bias).then_inc(d_bm, 16)
                m = mask[r:r + 1, :]
                sp.dma_start(msk[S * r:S * r + S, :, :],
                             bass.AP(m.tensor, m.offset, [[0, S], [2 * S, PAIRS], [1, S]])).then_inc(d_bm, 16)
            sp.dma_start(wf1[:, :], ffn1).then_inc(d_f1, 16)
            sp.wait_ge(s_T, UNITS)
            sp.dma_start(xs[:, :, D:ROW].bitcast(U32), tok_ids.rearrange("p (i c) -> p i c", c=4)).then_inc(d_tok, 16)
            sp.wait_ge(d_top, 16)
            sp.wait_ge(s_S, UNITS)
            for k in range(TOPK):
                i = sp.value_load(tki[0:1, k:k + 1], min_val=0, max_val=E - 1)
                sp.dma_start(lor[32 * k:32 * k + RANK, :], lora[bass.ds(i, 1), :, :].rearrange("a r n -> (a r) n"))\
                    .then_inc(d_lora, 16)
            sp.wait_ge(d_scat, 16 * TILES)
            for n in range(5):
                sp.dma_start(XS[:, 3 * n:3 * n + 3, :],
                             xs_dram[3 * n * P:(3 * n + 3) * P, :].rearrange("(j p) c -> p j c", p=P))\
                    .then_inc(d_xs, 16)
            sp.wait_ge(s_S, UNITS)
            sp.wait_ge(s_kt, 2 * CH)
            for h in range(H):
                r = slice(h * DK, (h + 1) * DK)
                sp.dma_start(Kx[r, h, :], KT[r, :]).then_inc(d_kx, 16)
            sp.wait_ge(d_yscat, 16 * SLOT_TILES)
            for c in range(CH):
                sp.dma_start(yg[:, tiles(c), :], y_dram.rearrange("(i p) d -> p i d", p=P)[:, tiles(c), :])\
                    .then_inc(d_yg, 16)
            for c in range(CH):
                sp.wait_ge(s_fin, c + 1)
                sp.dma_start(out.rearrange("(i p) d -> p i d", p=P)[:, tiles(c), :], xres[4][:, tiles(c), :])\
                    .then_inc(d_out, 16)
            sp.wait_ge(d_out, 16 * CH)

        @block.gpsimd
        def _(pool):
            links = [0]

            def link(ins):
                links[0] += 1
                ins.then_inc(g_chain, 1)
                pool.wait_ge(g_chain, links[0])

            pool.memset(Vx[:, :, :, :], 0.0).then_inc(s_zv, 1)
            pool.memset(nhalf[:, :], -0.5).then_inc(s_nh, 1)
            pool.wait_ge(s_nh, 1)

            def rstd_of(q, a, n):
                pool.wait_ge(s_ve_, stat_count(q, a))
                w = slice(a * TPP, (a + n) * TPP)
                pool.tensor_tensor(rstd[:, w], ve[:, w], nhalf[:, w], ALU.pow).then_inc(s_pow, 1)

            def residual_base(layer, c):
                pool.wait_ge(s_bo, layer + 1)
                if c == 0 and layer == 0:
                    pool.wait_ge(d_x, 32)
                if layer == 1:
                    pool.wait_ge(s_res, RES_X2 + c + 1)
                pool.tensor_tensor(xb[:, tiles(c), :], xres[2 * layer][:, tiles(c), :],
                                   mid_bcast(bo[:, :], TPC), ALU.add).then_inc(s_xb, 1)

            for c in range(CH):
                rstd_of(0, 2 * c, 2)
            pool.wait_ge(d_cst, 32)
            pool.wait_ge(s_kt, 2)
            for h in range(H):
                pool.tensor_tensor(Kx[:, h, cols(1)], KT[:, cols(1)],
                                   bass.AP(cst[:, HM + h:HM + h + 1].tensor, cst[:, HM + h:HM + h + 1].offset,
                                           [list(cst[:, HM + h:HM + h + 1].ap[0]), [0, TC]]), ALU.mult).then_inc(s_kx1, 1)
            for c in range(CH):
                residual_base(0, c)
            for a in range(PIECES):
                rstd_of(1, a, 1)
            pool.wait_ge(d_init, 16)
            pool.wait_ge(d_tok, 16)
            pool.wait_ge(s_slot, 1)
            pool.wait_ge(s_xs, 1)
            for i in range(TILES):
                pool.indirect_dma_start(out=xs_dram, out_offset=bass.IndirectOffsetOnAxis(ap=slot[:, i:i + 1], axis=0),
                                        in_=xs[:, i, :], in_offset=None).then_inc(d_scat, 16)
            for j in range(SLOT_TILES):
                pool.wait_ge(s_ys, j + 1)
                pool.indirect_dma_start(out=y_dram,
                                        out_offset=bass.IndirectOffsetOnAxis(ap=XS.bitcast(U32)[:, j, D:D + 1], axis=0),
                                        in_=ys[:, j, :], in_offset=None,
                                        bounds_check=T - 1, oob_is_err=False).then_inc(d_yscat, 16)
            for c in range(CH):
                rstd_of(2, 2 * c, 2)
            for u in range(UNITS + 5):
                if u < UNITS:
                    U = UNITS + u
                    pool.wait_ge(s_mx, u + 1)
                    pool.wait_ge(s_exp, U - 1)
                    pool.tensor_tensor(Sx[:, u % 2, :].rearrange("p (h k) -> p h k", h=HH),
                                       Sa[:, u % 2, :].rearrange("p (h k) -> p h k", h=HH),
                                       last_bcast(mx[:, u % 4, :], S), ALU.subtract).then_inc(s_sub, 1)
                if u in (0, 2):
                    residual_base(1, u // 2)
                if u in (9, 13, 17, 20):
                    rstd_of(3, (9, 13, 17, 20).index(u), 1)

        @block.scalar
        def _(act):
            act.dma_start(cst[:, :], consts).then_inc(d_cst, 16)
            act.dma_start(wat[0][:, :], att0).then_inc(d_att0, 16)
            act.dma_start(cstb[:, :].bitcast(mybir.dt.uint16), constb).then_inc(d_cst, 16)
            act.wait_ge(d_row, 16)
            act.activation(tg[:, :], row[:, GATES:GATES + 4], ACT.Tanh).then_inc(s_tg, 1)

            def k_evac(layer):
                for c in range(CH):
                    act.wait_ge(s_kp, CH * layer + c + 1)
                    if layer == 1 and c == 0:
                        act.wait_ge(s_kx0, H - ACT_HEADS)
                        act.wait_ge(s_kx1, H)
                    act.activation(KT[:, cols(c)], bank[(0, 3)[layer] + c][:, :], ACT.Identity,
                                   bias=wat[layer][:, BK:BK + 1]).then_inc(s_kt, 1)

            def normalise(q, a):
                act.wait_ge(s_nmr, stat_count(q, a))
                for i in range(a * TPP + (q + 1) % 2, (a + 1) * TPP):
                    ins = act.activation(xn[:, i, :], xres[q][:, i, :], ACT.Identity,
                                         bias=nmr[:, i:i + 1], scale=rstd[:, i:i + 1])
                ins.then_inc(s_xna, 1)

            def xnT_evac(q, a):
                act.wait_ge(s_xT, PIECES * q + a + 1)
                act.activation(xnT[:, cols(a, TPP * P)], bank[XT_BANK[q][a]][:, 0:TPP * P], ACT.Copy).then_inc(s_xnT, 1)

            def shared_tanh(n):
                act.wait_ge(s_shp, n + 1)
                if n >= 2:
                    act.wait_ge(s_shh, n - 1)
                act.activation(tnh[:, n % 2, :], bank[SH_BANKS[n][0]][:, :], ACT.Tanh, scale=0.5).then_inc(s_sht, 1)

            def relu1(s):
                act.wait_ge(s_z, s + 1)
                if s >= 2:
                    act.wait_ge(s_h1, s - 1)
                act.activation(r1[:, s % 2, :], bank[2 * (s % 3) + 1][:, :], ACT.Relu).then_inc(s_r1, 1)

            def attention(layer):
                for u in range(UNITS + 1):
                    U = UNITS * layer + u
                    if u < UNITS:
                        act.wait_ge(s_sub, U + 1)
                        if U >= 3:
                            act.wait_ge(s_T, U - 2)
                        act.activation(Pe[:, u % 3, :], Sx[:, u % 2, :], ACT.Exp).then_inc(s_exp, 1)
                    if u >= 1:
                        w = u - 1
                        act.wait_ge(s_T, U)
                        act.activation(PT[:, 4 * (w % 2):4 * (w % 2) + 4, cols(w // 2, P)],
                                       bank3(2 + w % 2, 4), ACT.Copy).then_inc(s_pt, 1)
                    q = 2 * layer + 1
                    if u == 11:
                        normalise(q, 0)
                    if u == 14:
                        xnT_evac(q, 0)
                    if u == 15:
                        normalise(q, 1)
                step = shared_tanh if layer == 0 else relu1
                xnT_evac(q, 1)
                step(0)
                normalise(q, 2)
                step(1)
                xnT_evac(q, 2)
                normalise(q, 3)
                xnT_evac(q, 3)

            k_evac(0)
            act.wait_ge(d_cst, 32)
            act.wait_ge(s_kt, 1)
            for a in (0, 1):
                normalise(0, a)
            for h in range(ACT_HEADS):
                hd = (h % 3) + 5 if h < 3 else (h % 3) + 13
                act.activation(Kx[:, hd, cols(0)], KT[:, cols(0)], ACT.Copy, scale=cst[:, HM + hd:HM + hd + 1])\
                    .then_inc(s_kxa, 1)
                if h == 2:
                    for a in (0, 1):
                        xnT_evac(0, a)
                    for a in (2, 3):
                        normalise(0, a)
            for a in (2, 3):
                xnT_evac(0, a)
            attention(0)
            act.wait_ge(s_lmax, 1)
            act.activation(th[:, :], lmax[:, :], ACT.Tanh, scale=0.5).then_inc(s_th, 1)
            shared_tanh(2)
            shared_tanh(3)
            k_evac(1)
            for j in range(SLOT_TILES + 2):
                if j < SLOT_TILES:
                    act.wait_ge(s_t1, j + 1)
                    if j >= 2:
                        act.wait_ge(s_gu, j - 1)
                    act.activation(xsT[:, j % 2, :], bank[j % 2][:, 0:P], ACT.Copy).then_inc(s_xsT, 1)
                if 1 <= j <= SLOT_TILES:
                    w = j - 1
                    act.wait_ge(s_gu, w + 1)
                    act.wait_ge(s_shh, 4)
                    if w >= 2:
                        act.wait_ge(s_rh, w - 1)
                    act.activation(tnh[:, w % 2, 0:F], bank[2 + w % 2][:, 0:F], ACT.Tanh, scale=0.5).then_inc(s_rt, 1)
                if j >= 2:
                    w = j - 2
                    act.wait_ge(s_t2, w + 1)
                    if w >= 2:
                        act.wait_ge(s_y, w - 1)
                    act.activation(hrT[:, w % 2, :], bank[4 + w % 2][:, 0:F], ACT.Copy).then_inc(s_hT, 1)
            for c in range(CH):
                for a in (2 * c, 2 * c + 1):
                    normalise(2, a)
                for a in (2 * c, 2 * c + 1):
                    xnT_evac(2, a)
            attention(1)
            for s in range(2, CH * FB1):
                relu1(s)

        @block.vector
        def _(dve):
            links = [0]

            def link(ins):
                links[0] += 1
                ins.then_inc(v_chain, 1)
                dve.wait_ge(v_chain, links[0])

            def stats(q, a, n):
                w = range(a * TPP, (a + n) * TPP)
                for i in w:
                    ins = dve.bn_stats(st[:, i, :], xres[q][:, i, :])
                link(ins)
                for i in w:
                    ins = dve.bn_aggr(mv[:, i, :], st[:, i, :])
                link(ins)
                w = slice(w[0], w[-1] + 1)
                dve.tensor_scalar(ve[:, w], mv[:, w, 1], EPS, None, ALU.add).then_inc(s_ve_, 1)

            def mean_rstd(q, a, n):
                dve.wait_ge(s_pow, stat_count(q, a))
                w = slice(a * TPP, (a + n) * TPP)
                dve.scalar_tensor_tensor(out=nmr[:, w], in0=mv[:, w, 0], scalar=-1.0,
                                         in1=rstd[:, w], op0=ALU.mult, op1=ALU.mult).then_inc(s_nmr, 1)

            def normalise(q, c):
                mean_rstd(q, 2 * c, 2)
                for a in (2 * c, 2 * c + 1):
                    i = a * TPP
                    dve.tensor_scalar(xn[:, i, :], xres[q][:, i, :], mv[:, i, 0:1], rstd[:, i:i + 1],
                                      ALU.subtract, ALU.mult).then_inc(s_xnv, 1)

            def bias_cols(layer):
                dve.tensor_scalar(bvb[:, :], ident, 0.0, wat[layer][:, BV:BV + 1], ALU.mult, ALU.add).then_inc(s_bvb, 1)

            def bias_out(layer):
                dve.wait_ge(s_ob, layer + 1)
                link(dve.tensor_tensor(bo[:, :], bank[OB_BANK[layer]][:, 0:D], row[:, (BO0, BO1)[layer]:(BO0, BO1)[layer] + D],
                                       ALU.add))
                dve.tensor_scalar(bo[:, :], bo[:, :], tg[:, layer:layer + 1], None, ALU.mult).then_inc(s_bo, 1)

            def v_evac(layer):
                for c in range(CH):
                    dve.wait_ge(s_vp, CH * layer + c + 1)
                    src = bank[V_BANK[layer][c]][:, :].rearrange("p (b a e d) -> p b a e d", b=HH, a=4, e=2)
                    for r in range(2):
                        for e in range(2):
                            o = (2 * e + r) * DK
                            ins = dve.tensor_copy(
                                Vx[S * r:S * r + S, c * HH:(c + 1) * HH, e::2, o:o + DK], src[S * r:S * r + S, :, :, e, :])
                    ins.then_inc(s_ve, 1)

            def q_evac(layer):
                for c in range(CH):
                    dve.wait_ge(s_qp, CH * layer + c + 1)
                    dve.tensor_scalar(QT[:, cols(c)], bank[Q_BANK[layer][c]][:, :], wat[layer][:, BQ:BQ + 1], SCALE,
                                      ALU.add, ALU.mult).then_inc(s_qt, 1)

            def unit(layer, u):
                U = UNITS * layer + u
                ps = bank3(u % 2, HH)
                dve.wait_ge(s_S, U + 1)
                if layer == 0:
                    link(dve.tensor_reduce(mx[:, u % 4, :], ps, AX.X, ALU.max))
                    if u >= 2:
                        dve.wait_ge(s_exp, U - 1)
                    dve.tensor_tensor(Sx[:, u % 2, :].rearrange("p (h k) -> p h k", h=HH), ps,
                                      last_bcast(mx[:, u % 4, :], S), ALU.subtract).then_inc(s_sub, 1)
                else:
                    sa = Sa[:, u % 2, :].rearrange("p (h k) -> p h k", h=HH)
                    if u >= 2:
                        dve.wait_ge(s_sub, U - 1)
                    dve.tensor_tensor(sa, ps, mid_bcast(bm[:, u // 2, :], HH), ALU.add).then_inc(s_add, 1)
                    dve.wait_ge(s_add, u + 1)
                    dve.tensor_reduce(mx[:, u % 4, :], sa, AX.X, ALU.max).then_inc(s_mx, 1)

            def norm(layer, bp):
                dve.wait_ge(s_av, PAIRS * layer + bp + 1)
                link(dve.reciprocal(oT[:, cols(bp, P)], bank[4 + bp % 2][:, P:2 * P]))
                dve.tensor_tensor(oT[:, cols(bp, P)], bank[4 + bp % 2][:, 0:P], oT[:, cols(bp, P)], ALU.mult)\
                    .then_inc(s_oT, 1)

            def residual(layer, a):
                dve.wait_ge(s_op, PAIRS * layer + TPP * (a + 1))
                dve.wait_ge(s_xb, CH * layer + a // 2 + 1)
                dve.scalar_tensor_tensor(out=xres[2 * layer + 1][:, piece(a), :],
                                         in0=bank[6][:, 0:TPP * D].rearrange("p (i d) -> p i d", i=TPP),
                                         scalar=tg[:, layer:layer + 1], in1=xb[:, piece(a), :],
                                         op0=ALU.mult, op1=ALU.add).then_inc(s_res, 1)
                dve.wait_ge(s_res, (0, RES_L1)[layer] + a + 1)
                stats(2 * layer + 1, a, 1)

            def attention(layer, step):
                q = 2 * layer + 1
                for bp in range(PAIRS):
                    unit(layer, 2 * bp)
                    if bp in (5, 7):
                        mean_rstd(q, (bp - 5) // 2, 1)
                    unit(layer, 2 * bp + 1)
                    if bp >= 2:
                        norm(layer, bp - 2)
                    if bp in (4, 6):
                        residual(layer, (bp - 4) // 2)
                norm(layer, 6)
                residual(layer, 2)
                step(0)
                norm(layer, 7)
                mean_rstd(q, 2, 1)
                residual(layer, 3)
                step(1)
                mean_rstd(q, 3, 1)

            def shared_step(n):
                c, f = n // 2, n % 2
                g, up = SH_BANKS[n]
                dve.wait_ge(s_sht, n + 1)
                link(dve.scalar_tensor_tensor(out=gac[:, n % 2, :], in0=tnh[:, n % 2, :], scalar=1.0,
                                              in1=bank[g][:, :], op0=ALU.add, op1=ALU.mult))
                dve.scalar_tensor_tensor(out=hsT[:, f, cols(c)], in0=gac[:, n % 2, :], scalar=0.5,
                                         in1=bank[up][:, :], op0=ALU.mult, op1=ALU.mult).then_inc(s_shh, 1)

            def ffn1_step(s):
                c, f = s // FB1, s % FB1
                dve.wait_ge(s_z, s + 1)
                link(dve.tensor_scalar(r0[:, s % 2, :], bank[2 * (s % 3)][:, :], 0.0, row[:, TOPV:TOPV + 1],
                                       ALU.max, ALU.mult))
                dve.wait_ge(s_r1, s + 1)
                dve.scalar_tensor_tensor(out=h1T[:, f, cols(c)], in0=r1[:, s % 2, :], scalar=row[:, TOPV + 1:TOPV + 2],
                                         in1=r0[:, s % 2, :], op0=ALU.mult, op1=ALU.add).then_inc(s_h1, 1)

            for c in range(CH):
                dve.wait_ge(d_x, 32)
                stats(0, 2 * c, 2)
            dve.wait_ge(d_cst, 32)
            dve.wait_ge(d_att0, 16)
            bias_cols(0)
            normalise(0, 0)
            mine = [h for h in range(H) if h not in (5, 6, 7, 13, 14, 15)]
            dve.wait_ge(s_kt, 1)
            for n, h in enumerate(mine):
                dve.tensor_scalar(Kx[:, h, cols(0)], KT[:, cols(0)], cst[:, HM + h:HM + h + 1], None, ALU.mult)\
                    .then_inc(s_kx0, 1)
                if n == 4:
                    normalise(0, 1)
            dve.wait_ge(s_zv, 1)
            v_evac(0)
            q_evac(0)
            dve.wait_ge(s_tg, 1)
            dve.wait_ge(d_row, 16)
            bias_out(0)
            attention(0, shared_step)

            dve.wait_ge(s_lg, 1)
            lg = bank[4][:, 0:TILES * E].rearrange("p (i e) -> p i e", e=E)
            dve.tensor_reduce(lmax[:, :], lg, AX.X, ALU.max).then_inc(s_lmax, 1)
            dve.wait_ge(s_lmax, 1)
            link(dve.tensor_tensor(eq[:, :, :], lg, last_bcast(lmax[:, :], E), ALU.is_equal))
            link(dve.tensor_tensor(wv[:, :, :], eq[:, :, :], mid_bcast(cst[:, W8:W8 + E], TILES), ALU.mult))
            link(dve.tensor_reduce(fmx[:, :], wv[:, :, :], AX.X, ALU.max))
            dve.tensor_tensor(oh[:, :, :], wv[:, :, :], last_bcast(fmx[:, :], E), ALU.is_equal).then_inc(s_oh, 1)
            dve.wait_ge(s_th, 1)
            link(dve.tensor_scalar(score[:, :], th[:, :], 0.5, 0.5, ALU.mult, ALU.add))
            dve.tensor_tensor(xs[:, :, 0:D], xn[:, :, :], last_bcast(score[:, :], D), ALU.mult).then_inc(s_xs, 1)
            dve.wait_ge(s_pre, 1)
            link(dve.tensor_tensor(cmp8[:, :, :], last_bcast(bank[2][:, 0:E], 8), mid_bcast(cst[:, THR:THR + 8], E),
                                   ALU.is_gt))
            link(dve.tensor_reduce(nt[:, :], cmp8[:, :, :], AX.X, ALU.add))
            link(dve.tensor_tensor(nt8[:, :, :], mid_bcast(nt[:, :], E),
                                   cst[:, TRI8:TRI8 + 64].rearrange("p (a b) -> p a b", a=E), ALU.mult))
            link(dve.tensor_reduce(base[:, :], nt8[:, :, :], AX.X, ALU.add))
            link(dve.scalar_tensor_tensor(out=sl[:, :, :], in0=mid_bcast(base[:, :], TILES), scalar=float(P),
                                          in1=bank[1][:, 0:TILES * E].rearrange("p (i e) -> p i e", e=E),
                                          op0=ALU.mult, op1=ALU.add))
            link(dve.tensor_tensor(slo[:, :, :], sl[:, :, :], oh[:, :, :], ALU.mult))
            link(dve.tensor_reduce(slotf[:, :], slo[:, :, :], AX.X, ALU.add))
            dve.tensor_copy(slot[:, :], slotf[:, :]).then_inc(s_slot, 1)
            link(dve.tensor_tensor(endt[:, :], base[:, :], nt[:, :], ALU.add))
            link(dve.tensor_tensor(tej[:, :, :], mid_bcast(endt[0:1, :], SLOT_TILES),
                                   last_bcast(cst[0:1, JT:JT + SLOT_TILES], E), ALU.is_le))
            link(dve.tensor_reduce(tef[:, :], tej[:, :, :], AX.X, ALU.add))
            dve.tensor_scalar(teo[:, :], tef[:, :], float(E - 1), float(2 * D), ALU.min, ALU.mult).then_inc(s_te, 1)

            shared_step(2)
            shared_step(3)
            for c in range(CH):
                dve.wait_ge(s_sdn, c + 1)
                dve.scalar_tensor_tensor(out=xb[:, tiles(c), :], in0=bank3((2, 3)[c], TPC), scalar=tg[:, 2:3],
                                         in1=xres[1][:, tiles(c), :], op0=ALU.mult, op1=ALU.add).then_inc(s_shr, 1)
            dve.wait_ge(d_att1, 16)
            bias_cols(1)
            v_evac(1)
            bias_out(1)
            dve.wait_ge(d_bm, 64)
            link(dve.tensor_scalar(bm[:, :, :], msk[:, :, :], NEG, None, ALU.mult))
            link(dve.tensor_tensor(bm[:, :, :], bm[:, :, :], mid_bcast(bia[:, :], PAIRS), ALU.add))
            for j in range(SLOT_TILES + 2):
                if j < SLOT_TILES:
                    g = bank[2 + j % 2]
                    dve.wait_ge(s_rt, j + 1)
                    link(dve.scalar_tensor_tensor(out=gac[:, j % 2, 0:F], in0=tnh[:, j % 2, 0:F], scalar=1.0,
                                                  in1=g[:, 0:F], op0=ALU.add, op1=ALU.mult))
                    if j >= 2:
                        dve.wait_ge(s_t2, j - 1)
                    dve.scalar_tensor_tensor(out=hr[:, j % 2, :], in0=gac[:, j % 2, 0:F], scalar=0.5,
                                             in1=g[:, F:2 * F], op0=ALU.mult, op1=ALU.mult).then_inc(s_rh, 1)
                if j >= 2:
                    w = j - 2
                    dve.wait_ge(s_y, w + 1)
                    dve.tensor_copy(ys[:, w, :], bank[6 + w % 2][:, 0:D]).then_inc(s_ys, 1)
            for k in range(TOPK):
                dve.wait_ge(s_wl, k + 1)
                if k == 0:
                    dve.wait_ge(d_f1, 16)
                dve.tensor_tensor(weff[:, k, :], bank[4 + k][:, :], wf1[:, 0:F1], ALU.add).then_inc(s_we, 1)
            for c in range(CH):
                dve.wait_ge(d_yg, 32)
                dve.scalar_tensor_tensor(out=xres[2][:, tiles(c), :], in0=yg[:, tiles(c), :], scalar=tg[:, 2:3],
                                         in1=xb[:, tiles(c), :], op0=ALU.mult, op1=ALU.add).then_inc(s_res, 1)
                dve.wait_ge(s_res, RES_X2 + c + 1)
                stats(2, 2 * c, 2)
            for c in range(CH):
                normalise(2, c)
            q_evac(1)
            attention(1, ffn1_step)
            for s in range(2, CH * FB1):
                ffn1_step(s)
            for c in range(CH):
                dve.wait_ge(s_dn, c + 1)
                dve.scalar_tensor_tensor(out=xres[4][:, tiles(c), :], in0=bank3(6 + c, TPC), scalar=tg[:, 3:4],
                                         in1=xres[3][:, tiles(c), :], op0=ALU.mult, op1=ALU.add).then_inc(s_fin, 1)

        @block.tensor
        def _(pe):
            def mm(o, l, r, first=True, last=True, **k):
                return pe.matmul(o, l, r, start=first, stop=last, **k)

            def k_proj(layer):
                for c in range(CH):
                    mm(bank[(0, 3)[layer] + c][:, :], wat[layer][:, WK:WK + D], ctxT[:, cols(c)]).then_inc(s_kp, 1)

            def v_proj(layer):
                wvt = wat[layer][:, WV:WV + D].rearrange("p (a r d) -> p r a d", r=2, d=DK)
                for c in range(CH):
                    for n in range(HH):
                        b = c * HH + n
                        for r in range(2):
                            o = bank[V_BANK[layer][c]][S * r:S * r + S, n * S:(n + 1) * S]
                            ins = mm(o.rearrange("p (a d) -> p a d", d=DK), ctxT[:, b * S:(b + 1) * S], wvt[:, r])
                    ins.then_inc(s_vp, 1)

            def out_bias(layer):
                pe.wait_ge(s_bvb, layer + 1)
                mm(bank[OB_BANK[layer]][:, 0:D], bvb[:, :], wat[layer][:, WO:WO + D]).then_inc(s_ob, 1)

            def xn_transpose(q, a):
                n = PIECES * q + a + 1
                if q % 2:
                    if a:
                        pe.wait_ge(s_xnT, n - 1)
                else:
                    pe.wait_ge(s_xnv, PIECES * (q // 2) + a + 1)
                pe.wait_ge(s_xna, n)
                for k in range(TPP):
                    ins = pe.transpose(bank[XT_BANK[q][a]][:, k * P:(k + 1) * P], xn[:, a * TPP + k, :], ident)
                ins.then_inc(s_xT, 1)

            def q_proj(layer, c):
                pe.wait_ge(s_xnT, PIECES * 2 * layer + 2 * c + 2)
                if layer == 0:
                    pe.wait_ge(s_kt, c + 1)
                mm(bank[Q_BANK[layer][c]][:, :], wat[layer][:, WQ:WQ + D], xnT[:, cols(c)]).then_inc(s_qp, 1)

            def scores(layer, u):
                U = UNITS * layer + u
                bp, hh = u // 2, u % 2
                if u >= 2:
                    if layer == 0:
                        pe.wait_ge(s_sub, U - 1)
                    else:
                        pe.wait_ge(s_add, u - 1)
                for r in range(2):
                    b = 2 * bp + r
                    ins = mm(bank[u % 2][S * r:S * r + S, :].rearrange("p (h k) -> p h k", h=HH),
                             QT[:, b * S:(b + 1) * S], Kx[:, HH * hh:HH * (hh + 1), b * S:(b + 1) * S])
                ins.then_inc(s_S, 1)

            def transposes(layer, u):
                U = UNITS * layer + u
                pe.wait_ge(s_exp, U + 1)
                if U >= 2:
                    pe.wait_ge(s_pt, U - 1)
                for m in range(4):
                    ins = pe.transpose(bank[2 + u % 2][:, m * P:(m + 1) * P], Pe[:, u % 3, m * P:(m + 1) * P], ident)
                ins.then_inc(s_T, 1)

            def values(layer, bp):
                pe.wait_ge(s_pt, UNITS * layer + 2 * bp + 2)
                if bp >= 2:
                    pe.wait_ge(s_oT, PAIRS * layer + bp - 1)
                o = bank[4 + bp % 2]
                for e in range(2):
                    for g in range(4):
                        a = 2 * g + e
                        mm(o[32 * g:32 * g + 32, P:2 * P], onesx[:, e, :],
                           PT[:, a, bp * P:(bp + 1) * P], first=(e == 0), last=(e == 1), tile_position=(0, 32 * g))
                for r in range(2):
                    b = 2 * bp + r
                    for e in range(2):
                        for g in range(4):
                            a = 2 * g + e
                            ins = mm(o[32 * g:32 * g + 32, S * r:S * r + S], Vx[:, b, a, :],
                                     PT[:, a, b * S:(b + 1) * S], first=(e == 0), last=(e == 1), tile_position=(0, 32 * g))
                ins.then_inc(s_av, 1)

            def out_proj(layer, bp):
                pe.wait_ge(s_oT, PAIRS * layer + bp + 1)
                if bp % TPP == 0 and bp:
                    pe.wait_ge(s_res, (0, RES_L1)[layer] + bp // TPP)
                k = bp % TPP
                mm(bank[6][:, k * D:(k + 1) * D], oT[:, bp * P:(bp + 1) * P], wat[layer][:, WO:WO + D]).then_inc(s_op, 1)

            def attention(layer, step):
                q = 2 * layer + 1
                if layer == 1:
                    pe.wait_ge(d_kx, 16 * H)
                for c in range(CH):
                    pe.wait_ge(s_ve, CH * layer + c + 1)
                for bp in range(PAIRS + 1):
                    if bp % (PAIRS // CH) == 0 and bp < PAIRS:
                        c = bp // (PAIRS // CH)
                        pe.wait_ge(s_qt, CH * layer + c + 1)
                        if layer == 0 and c == 0:
                            pe.wait_ge(s_kx0, H - ACT_HEADS)
                            pe.wait_ge(s_kxa, ACT_HEADS)
                        if layer == 0 and c == 1:
                            pe.wait_ge(s_kx1, H)
                    for hh in range(2):
                        if bp < PAIRS:
                            scores(layer, 2 * bp + hh)
                        if bp >= 1:
                            transposes(layer, 2 * bp - 2 + hh)
                    if bp >= 2:
                        values(layer, bp - 2)
                    if bp >= 3:
                        out_proj(layer, bp - 3)
                    if bp == 7:
                        xn_transpose(q, 0)
                xn_transpose(q, 1)
                step(0)
                values(layer, 7)
                out_proj(layer, 6)
                step(1)
                xn_transpose(q, 2)
                out_proj(layer, 7)
                return q

            pe.wait_ge(d_ctx, 16)
            pe.wait_ge(d_att0, 16)
            k_proj(0)
            v_proj(0)
            pe.wait_ge(d_cst, 32)
            for c in range(CH):
                for a in (2 * c, 2 * c + 1):
                    xn_transpose(0, a)
                q_proj(0, c)
            pe.wait_ge(s_ve, 1)
            out_bias(0)
            pe.wait_ge(s_bo, 1)

            def shared_up(n):
                c, f = n // 2, n % 2
                if n == 0:
                    pe.wait_ge(d_sh, 16)
                    pe.wait_ge(s_sub, UNITS)
                if n == 1:
                    pe.wait_ge(s_pt, UNITS)
                if n == 2:
                    pe.wait_ge(s_oT, PAIRS)
                if n == 3:
                    pe.wait_ge(s_shh, 1)
                pe.wait_ge(s_xnT, PIECES + 2 * c + 2)
                for k in range(2):
                    ins = mm(bank[SH_BANKS[n][k]][:, :], wsh[:, k * F + f * P:k * F + (f + 1) * P], xnT[:, cols(c)])
                ins.then_inc(s_shp, 1)

            def ffn1_up(s):
                c, f = s // FB1, s % FB1
                pe.wait_ge(s_xnT, PIECES * 3 + 2 * c + 2)
                if s == 0:
                    pe.wait_ge(s_we, TOPK)
                    pe.wait_ge(s_add, UNITS)
                if s == 1:
                    pe.wait_ge(s_pt, 2 * UNITS)
                if s == 2:
                    pe.wait_ge(s_oT, 2 * PAIRS)
                if s >= 3:
                    pe.wait_ge(s_h1, s - 2)
                for k in range(TOPK):
                    ins = mm(bank[2 * (s % 3) + k][:, :], weff[:, k, f * P:(f + 1) * P], xnT[:, cols(c)])
                ins.then_inc(s_z, 1)

            attention(0, shared_up)

            def logits(i):
                return mm(bank[4][:, i * E:(i + 1) * E], xnT[:, i * P:(i + 1) * P], wat[0][:, WGATE:WGATE + E])

            for a in range(PIECES):
                if a == 3:
                    xn_transpose(1, 3)
                pe.wait_ge(s_xnT, PIECES + a + 1)
                for i in range(a * TPP, (a + 1) * TPP):
                    ins = logits(i)
            ins.then_inc(s_lg, 1)
            shared_up(2)
            pe.wait_ge(s_oh, 1)
            pe.wait_ge(s_shh, 2)
            mm(bank[1][:, 0:TILES * E], tri, oh[:, :, :].rearrange("p i e -> p (i e)"), skip_group_check=True)
            for s in range(1, TILES):
                mm(bank[1][:, s * E:TILES * E], ones_bf, oh[:, 0:TILES - s, :].rearrange("p i e -> p (i e)"),
                   first=False, skip_group_check=True)
            for i in range(TILES):
                ins = mm(bank[2][:, 0:E], ones_bf, oh[:, i, :], first=(i == 0), last=(i == TILES - 1))
            ins.then_inc(s_pre, 1)
            shared_up(3)
            for c in range(CH):
                pe.wait_ge(s_shh, (2, 4)[c])
                pe.wait_ge(s_slot, 1)
                for i in range(TPC):
                    t = c * TPC + i
                    for f in range(2):
                        ins = mm(bank[2 + c][:, i * D:(i + 1) * D], hsT[:, f, t * P:(t + 1) * P],
                                 wsh[:, 2 * F + f * D:2 * F + (f + 1) * D], first=(f == 0), last=(f == 1))
                ins.then_inc(s_sdn, 1)
            pe.wait_ge(d_att1, 16)
            pe.wait_ge(s_shr, CH)
            pe.wait_ge(s_te, 1)
            k_proj(1)
            v_proj(1)
            out_bias(1)

            pe.wait_ge(d_rgu, 16)
            pe.wait_ge(d_rdn, 16)
            pe.wait_ge(s_ve, 2 * CH)
            pe.wait_ge(s_bo, 2)
            pe.wait_ge(s_kt, 2 * CH)
            pe.wait_ge(s_shr, CH)
            first_col = {}
            for j in range(SLOT_TILES + 3):
                if j < SLOT_TILES:
                    if j % 3 == 0:
                        pe.wait_ge(d_xs, 16 * 5 if j else 16 * 5)
                    if j >= 2:
                        pe.wait_ge(s_xsT, j - 1)
                    pe.transpose(bank[j % 2][:, 0:P], XS[:, j, 0:D], ident).then_inc(s_t1, 1)
                if 1 <= j <= SLOT_TILES:
                    w = j - 1
                    e = pe.value_load(teo[0:1, w:w + 1], min_val=0, max_val=(E - 1) * 2 * D)
                    first_col[w] = e
                    pe.wait_ge(s_xsT, w + 1)
                    if w >= 2:
                        pe.wait_ge(s_rh, w - 1)
                    mm(bank[2 + w % 2][:, :], xsT[:, w % 2, :], wgu[:, bass.ds(e * 2, 2 * F)]).then_inc(s_gu, 1)
                if 2 <= j <= SLOT_TILES + 1:
                    w = j - 2
                    pe.wait_ge(s_rh, w + 1)
                    if w >= 2:
                        pe.wait_ge(s_hT, w - 1)
                    for f in range(2):
                        ins = pe.transpose(bank[4 + w % 2][:, f * P:(f + 1) * P], hr[:, w % 2, f * P:(f + 1) * P], ident)
                    ins.then_inc(s_t2, 1)
                if j >= 3:
                    w = j - 3
                    e = first_col[w]
                    pe.wait_ge(s_hT, w + 1)
                    if w >= 2:
                        pe.wait_ge(s_ys, w - 1)
                    for f in range(2):
                        ins = mm(bank[6 + w % 2][:, 0:D], hrT[:, w % 2, f * P:(f + 1) * P],
                                 wdn[:, bass.ds(e + f * D, D)], first=(f == 0), last=(f == 1))
                    ins.then_inc(s_y, 1)
            pe.wait_ge(d_lora, 32)
            pe.wait_ge(s_hT, SLOT_TILES)
            for k in range(TOPK):
                r = slice(32 * k, 32 * k + RANK)
                mm(bank[4 + k][:, :], lor[r, 0:D], lor[r, D:D + F1]).then_inc(s_wl, 1)

            for c in range(CH):
                for a in (2 * c, 2 * c + 1):
                    xn_transpose(2, a)
                q_proj(1, c)
            attention(1, ffn1_up)
            for s in range(2, CH * FB1 + 1):
                if s == 2:
                    ffn1_up(2)
                    xn_transpose(3, 3)
                elif s < CH * FB1:
                    ffn1_up(s)
                if s >= 1 and (s - 1) % FB1 == FB1 - 1:
                    c = (s - 1) // FB1
                    pe.wait_ge(s_h1, (c + 1) * FB1)
                    for i in range(TPC):
                        t = c * TPC + i
                        for f in range(FB1):
                            ins = mm(bank[6 + c][:, i * D:(i + 1) * D], h1T[:, f, t * P:(t + 1) * P],
                                     wf1[:, F1 + f * D:F1 + (f + 1) * D], first=(f == 0), last=(f == FB1 - 1))
                    ins.then_inc(s_dn, 1)


_ORDER = ["x_in", "ctx_in", "att0", "att1", "consts", "constb", "rows", "shared", "rgu", "rdn", "ffn1", "lora",
          "topi", "bias", "mask", "tok_ids", "slot_init"]


def pack(a):
    import numpy as np

    def col(v):
        return v.reshape(-1, 1)

    wi, bi = a["L1_xattn_in_proj_w"], a["L1_xattn_in_proj_b"]
    consts = np.zeros((P, CONST_COLS), np.float32)
    consts[:, ID:ID + P] = np.eye(P)
    for p in range(P):
        for e in range(2):
            o = ONESX + 32 * e + (2 * e + p // S) * DK
            consts[p, o:o + DK] = 1.0
    consts[:, W8:W8 + E] = np.arange(E, 0, -1)
    consts[:, THR:THR + 8] = np.arange(8) * P
    consts[:, TRI8:TRI8 + 64] = np.tril(np.ones((E, E)), -1).reshape(-1)
    consts[:, JT:JT + 16] = np.arange(16)
    consts[np.arange(P), HM + np.arange(P) // DK] = 1.0
    one = 0x3F80
    constb = np.full((P, 2 * P), one, np.uint16)
    constb[:, 0:P] = np.triu(np.ones((P, P)), 1).astype(np.uint16) * one
    tok = np.zeros((P, TILES, 4), np.uint32)
    tok[:, :, 0] = np.arange(TILES)[None, :] * P + np.arange(P)[:, None]
    init = np.zeros((SLOT_TILES * P, ROW), np.uint32)
    init[:, D] = 4 * T + np.arange(SLOT_TILES * P)
    pad = np.zeros((D, E), np.float32)
    return {
        "x_in": a["x"].reshape(T, D),
        "ctx_in": a["ctx_1024"].reshape(T, D).T,
        "att0": np.concatenate([a["L0_xattn_Wk"].T, a["L0_xattn_Wv"].T, col(a["L0_xattn_bk"]), col(a["L0_xattn_bv"]),
                                col(a["L0_xattn_bq"]), a["L0_xattn_Wq"].T, a["L0_xattn_Wo"].T,
                                a["L0_ffn_gate_w"].T], 1),
        "att1": np.concatenate([wi[D:2 * D].T, wi[2 * D:].T, col(bi[D:2 * D]), col(bi[2 * D:]), col(bi[:D]),
                                wi[:D].T, a["L1_xattn_out_proj_w"].T, pad], 1),
        "consts": consts,
        "constb": constb,
        "rows": np.concatenate([a["L0_xattn_bo"], a["L1_xattn_out_proj_b"], a["g_xattn"], a["g_ffn"],
                                a["L1_ffn_top_k_values"]]).reshape(1, -1),
        "shared": np.concatenate([a["L0_ffn_shared_gate"].T, a["L0_ffn_shared_up"].T,
                                  a["L0_ffn_shared_down"].T.reshape(2, P, D).transpose(1, 0, 2).reshape(P, 2 * D)], 1),
        "rgu": np.stack([a["L0_ffn_r_gate"].transpose(2, 0, 1), a["L0_ffn_r_up"].transpose(2, 0, 1)], 2)
                 .reshape(D, E * 2 * F),
        "rdn": a["L0_ffn_r_down"].transpose(2, 0, 1).reshape(2, P, E, D).transpose(1, 2, 0, 3).reshape(P, E * 2 * D),
        "ffn1": np.concatenate([a["L1_ffn_wi_w"].T,
                                a["L1_ffn_wo_w"].T.reshape(FB1, P, D).transpose(1, 0, 2).reshape(P, F1)], 1),
        "lora": np.concatenate([a["L1_ffn_lora_As"], a["L1_ffn_lora_Bs"].transpose(0, 2, 1)], 2),
        "topi": a["L1_ffn_top_k_indices"].reshape(1, TOPK),
        "bias": a["fside_1xSxS2_0"][0],
        "mask": a["mask_BxS2_bk0"],
        "tok_ids": tok.reshape(P, TILES * 4),
        "slot_init": init.view(np.float32),
    }


def kernel(**inputs):
    import numpy as _np
    import concourse.bacc as _bacc
    from concourse import mybir as _mybir
    from concourse.bass_utils import run_bass_kernel_spmd as _run

    nc = _bacc.Bacc("TRN2", target_bir_lowering=False, num_devices=1)
    packed = pack({k: _np.asarray(v) for k, v in inputs.items()})
    arrays, args = {}, []
    for name in _ORDER:
        a = _np.ascontiguousarray(packed[name])
        arrays[name] = a
        args.append(nc.dram_tensor(name, a.shape, _mybir.dt.from_np(a.dtype), kind="ExternalInput").ap())
    out = nc.dram_tensor("out", (T, D), F32, kind="ExternalOutput").ap()
    build(nc, *args, out)
    r = _run(nc, [arrays], core_ids=[0])
    return r.results[0]["out"].reshape(B, S, D)
```

```python
from contextlib import ExitStack

import concourse.bass as bass
from concourse import mybir

F32 = mybir.dt.float32
BF16 = mybir.dt.bfloat16
U32 = mybir.dt.uint32
I32 = mybir.dt.int32
ALU = mybir.AluOpType
ACT = mybir.ActivationFunctionType
AX = mybir.AxisListType

B, S, D = 16, 64, 128
H, DK = 16, 8
T = B * S
P = 128
TILES = T // P
CH = 2
TPC = TILES // CH
TC = T // CH
PIECES = 4
TPP = TILES // PIECES
PAIRS = B // 2
UNITS = PAIRS * 2
HH = H // 2
HP = H // 2
E, F = 8, 256
SLOT_TILES = TILES + E - 1
ROW_TILES = E * TILES + SLOT_TILES - TILES
GROUPS = [(0, 4), (4, 8)]
ROW = D + 4
F1 = 512
FB1 = F1 // P
RANK, TOPK = 16, 2
SCALE = DK ** -0.5
EPS = 1e-5
NEG = -3.4028234663852886e38

WK, WV, BK, BV, BQ = 0, D, 2 * D, 2 * D + 1, 2 * D + 2
WQ, WO, WGATE = 2 * D + 3, 3 * D + 3, 4 * D + 3
ATT_COLS = 4 * D + 3 + E
ID, ONESX, W8, THR, TRI8, JT = 0, 128, 192, 200, 208, 272
HM = JT + 16
REG, JP = HM + H // 2, HM + H // 2 + E
CONST_COLS = JP + 16
BO0, BO1, GATES, TOPV = 0, D, 2 * D, 2 * D + 4
ROW_COLS = 2 * D + 4 + TOPK


def last_bcast(ap, n):
    return bass.AP(ap.tensor, ap.offset, [list(d) for d in ap.ap] + [[0, n]])


def mid_bcast(ap, n):
    dims = [list(d) for d in ap.ap]
    return bass.AP(ap.tensor, ap.offset, dims[:1] + [[0, n]] + dims[1:])


def build(nc, x_in, ctx_in, att0, att1, consts, constb, rows, shared, rgu, rdn, ffn1, lora, topi,
          bias, mask, tok_ids, empty_in, out):
    with ExitStack() as ctx:
        def sb(name, shape, dt=F32):
            return ctx.enter_context(nc.sbuf_tensor(name, shape, dt))

        def sem(name):
            return ctx.enter_context(nc.semaphore(name))

        bank = [ctx.enter_context(nc.psum_tensor(f"bank{i}", [P, 512], F32)) for i in range(8)]
        xs_dram = nc.dram_tensor("sorted_rows", [ROW_TILES * P, ROW], F32).ap()
        y_dram = nc.dram_tensor("routed_rows", [T, D], F32).ap()

        ctxT = sb("ctxT", [P, T])
        wat = [sb("wat0", [P, ATT_COLS]), sb("wat1", [P, ATT_COLS])]
        cst = sb("cst", [P, CONST_COLS])
        cstb = sb("cstb", [P, 2 * P], BF16)
        row = sb("row", [P, ROW_COLS])
        wsh = sb("wsh", [P, 3 * F])
        wgu = sb("wgu", [P, E * 2 * F])
        wdn = sb("wdn", [P, E * 2 * D])
        wf1 = sb("wf1", [P, 2 * F1])
        tki = sb("tki", [1, TOPK], I32)
        msk = sb("msk", [P, PAIRS, S], mybir.dt.uint8)
        bia = sb("bia", [P, S])
        empty = sb("empty", [P, ROW])
        bm = wsh[:, 0:PAIRS * S].rearrange("p (a k) -> p a k", a=PAIRS)
        tg = sb("tg", [P, 4])
        zb = sb("zb", [P, 32], BF16)
        xr = [sb(f"xr{i}", [P, TILES, D]) for i in range(2)]
        xres = [xr[0], xr[1], xr[0], xr[1], xr[0]]
        xb = sb("xb", [P, TILES, D])
        xn = sb("xn", [P, TILES, D])
        xnT = sb("xnT", [P, T])
        st = sb("st", [P, TILES, 6])
        mv = sb("mv", [P, TILES, 2])
        ve = sb("ve", [P, TILES])
        nhalf = sb("nhalf", [P, TILES])
        rstd = sb("rstd", [P, TILES])
        nmr = sb("nmr", [P, TILES])
        KT = sb("KT", [P, T])
        QT = sb("QT", [P, 2, T])
        lor = QT[:, 0, 0:D + F1]
        oT = sb("oT", [P, T])
        Kx = sb("Kx", [P, HH, T])
        Vx = sb("Vx", [P, B, HP, 32])
        Sa = sb("Sa", [P, 2, HH * S])
        Sx = sb("Sx", [P, 2, HH * S])
        Pe = sb("Pe", [P, 3, HH * S])
        mx = sb("mx", [P, 4, HH])
        bvb = sb("bvb", [P, D])
        bo = sb("bo", [P, D])
        big = sb("big", [P, HP * T])
        PT = big[:, :].rearrange("p (a t) -> p a t", a=HP)
        hsT = big[:, 0:2 * T].rearrange("p (f t) -> p f t", f=2)
        XS = big[:, 2 * T:2 * T + SLOT_TILES * ROW].rearrange("p (j c) -> p j c", c=ROW)
        o = 2 * T + SLOT_TILES * ROW
        ys = big[:, o:o + SLOT_TILES * D].rearrange("p (j c) -> p j c", c=D)
        yg = big[:, o + SLOT_TILES * D:o + SLOT_TILES * D + T].rearrange("p (i c) -> p i c", c=D)
        h1T = big[:, 0:FB1 * T].rearrange("p (f t) -> p f t", f=FB1)
        r0 = big[:, FB1 * T:FB1 * T + 2 * TC].rearrange("p (a t) -> p a t", a=2)
        r1 = big[:, FB1 * T + 2 * TC:FB1 * T + 4 * TC].rearrange("p (a t) -> p a t", a=2)
        weff = wgu[:, 0:TOPK * F1].rearrange("p (k f) -> p k f", k=TOPK)
        eq = sb("eq", [P, TILES, E])
        wv = sb("wv", [P, TILES, E])
        lmax = sb("lmax", [P, TILES])
        fmx = sb("fmx", [P, TILES])
        oh = sb("oh", [P, TILES, E], BF16)
        th = sb("th", [P, TILES])
        score = sb("score", [P, TILES])
        cmp8 = sb("cmp8", [P, E, 8])
        nt = sb("nt", [P, E])
        nt8 = sb("nt8", [P, E, 8])
        base = sb("base", [P, E])
        endt = sb("endt", [P, E])
        sl = sb("sl", [P, TILES, E])
        slo = sb("slo", [P, TILES, E])
        slotf = sb("slotf", [P, TILES])
        slot = sb("slot", [P, TILES], U32)
        tej = sb("tej", [1, SLOT_TILES, E])
        tef = sb("tef", [1, SLOT_TILES])
        teo = sb("teo", [1, SLOT_TILES], I32)
        tbj = sb("tbj", [1, SLOT_TILES, E])
        tbf = sb("tbf", [1, SLOT_TILES])
        row0f = sb("row0f", [1, SLOT_TILES])
        row0 = sb("row0", [1, SLOT_TILES], I32)
        xs = Pe[:, :, :].rearrange("p a b -> p (a b)")[:, 0:TILES * ROW].rearrange("p (i c) -> p i c", c=ROW)
        tnh, gac = Sa, Sx
        xsT = sb("xsT", [P, 2, P])
        o = o + SLOT_TILES * D + T
        hr = big[:, o:o + 2 * F].rearrange("p (a f) -> p a f", a=2)
        hrT = big[:, o + 2 * F:o + 4 * F].rearrange("p (a f) -> p a f", a=2)

        ident = cst[:, ID:ID + P]
        onesx = cst[:, ONESX:ONESX + 64].rearrange("p (a c) -> p a c", a=2)
        tri, ones_bf = cstb[:, 0:P], cstb[:, P:2 * P]

        d_att0, d_att1, d_cst, d_row = map(sem, ("d_att0", "d_att1", "d_cst", "d_row"))
        d_ctx, d_x = [sem(f"d_ctx{c}") for c in range(CH)], [sem(f"d_x{c}") for c in range(CH)]
        d_sh, d_rgu, d_rdn, d_f1, d_bm, d_top, d_lora = map(
            sem, ("d_sh", "d_rgu", "d_rdn", "d_f1", "d_bm", "d_top", "d_lora"))
        d_empty, d_tok, d_init, d_kx, d_scat, d_yscat, d_out = map(
            sem, ("d_empty", "d_tok", "d_init", "d_kx", "d_scat", "d_yscat", "d_out"))
        d_yg = [sem(f"d_yg{a}") for a in range(PIECES)]
        d_xs = [sem(f"d_xs{i}") for i in range(SLOT_TILES)]
        s_zq, s_zv, s_nh, s_kx0, s_kx1, s_kxa = map(sem, ("s_zq", "s_zv", "s_nh", "s_kx0", "s_kx1", "s_kxa"))
        v_chain, a_chain, g_chain = sem("v_chain"), sem("a_chain"), sem("g_chain")
        s_tg, s_bvb, s_ob, s_bo, s_xb = map(sem, ("s_tg", "s_bvb", "s_ob", "s_bo", "s_xb"))
        s_kp, s_kt, s_vp, s_ve, s_qp, s_qt = map(sem, ("s_kp", "s_kt", "s_vp", "s_ve", "s_qp", "s_qt"))
        s_ve_, s_pow, s_nmr, s_xnv, s_xna, s_xT, s_xnT = map(
            sem, ("s_var", "s_pow", "s_nmr", "s_xnv", "s_xna", "s_xT", "s_xnT"))
        s_S, s_add, s_mx, s_sub, s_exp, s_T, s_pt, s_av, s_oT, s_op, s_res = map(
            sem, ("s_S", "s_add", "s_mx", "s_sub", "s_exp", "s_T", "s_pt", "s_av", "s_oT", "s_op", "s_res"))
        s_zb = sem("s_zb")
        s_lg, s_lmax, s_th, s_oh, s_pre, s_slot, s_te, s_xs = map(
            sem, ("s_lg", "s_lmax", "s_th", "s_oh", "s_pre", "s_slot", "s_te", "s_xs"))
        s_shp, s_sht, s_shh, s_sdn, s_shr = map(sem, ("s_shp", "s_sht", "s_shh", "s_sdn", "s_shr"))
        s_t1, s_xsT, s_gu, s_rt, s_rh, s_t2, s_hT, s_y, s_ys = map(
            sem, ("s_t1", "s_xsT", "s_gu", "s_rt", "s_rh", "s_t2", "s_hT", "s_y", "s_ys"))
        s_wl, s_we, s_z, s_r1, s_h1, s_dn, s_fin = map(
            sem, ("s_wl", "s_we", "s_z", "s_r1", "s_h1", "s_dn", "s_fin"))
        XT_BANK = [(2, 3, 4, 5), (7,) * 4, (2, 3, 6, 7), (7,) * 4]
        K_BANK, V_BANK = [(0, 1), (0, 1)], [(6, 7), (0, 1)]
        Q_BANK = XT_BANK[0::2]
        OB_BANK = (7, 2)
        SH_BANKS = [(0, 1), (3, 5), (0, 1), (6, 7)]
        SD_BANK = (3, 5)
        EARLY = 5
        DN_BANK = (6, 7, 0, 1)
        LG_BANK = (2, 4)
        ACT_HEADS = 3
        RES_X2, RES_L1 = PIECES, 2 * PIECES
        block = ctx.enter_context(nc.Block())

        def tiles(c):
            return slice(c * TPC, (c + 1) * TPC)

        def cols(c, n=TC):
            return slice(c * n, (c + 1) * n)

        def piece(a):
            return slice(a * TPP, (a + 1) * TPP)

        def stat_count(q, a):
            return PIECES * q + a + 1

        def bank3(i, n):
            return bank[i][:, 0:n * (512 // n)].rearrange("p (a b) -> p a b", a=n)

        @block.sync
        def _(sp):
            for c in range(CH):
                sp.dma_start(ctxT[:, cols(c)], ctx_in[:, cols(c)]).then_inc(d_ctx[c], 16)
                sp.dma_start(xr[0][:, tiles(c), :], x_in.rearrange("(i p) d -> p i d", p=P)[:, tiles(c), :])\
                    .then_inc(d_x[c], 16)
            sp.dma_start(row[:, :], bass.AP(rows.tensor, rows.offset, [[0, P], [1, ROW_COLS]])).then_inc(d_row, 16)
            sp.dma_start(tki[:, :], topi).then_inc(d_top, 16)
            sp.dma_start(empty[:, :], empty_in).then_inc(d_empty, 16)
            sp.dma_start(wsh[:, :], shared).then_inc(d_sh, 16)
            sp.dma_start(wgu[:, :], rgu).then_inc(d_rgu, 16)
            sp.dma_start(wdn[:, :], rdn).then_inc(d_rdn, 16)
            sp.wait_ge(d_empty, 16)
            e = empty[:, :]
            sp.dma_start(xs_dram.rearrange("(k p) c -> p k c", p=P),
                         bass.AP(e.tensor, e.offset, [list(e.ap[0]), [0, ROW_TILES], [1, ROW]])).then_inc(d_init, 16)
            sp.dma_start(wat[1][:, :], att1).then_inc(d_att1, 16)
            for r in range(2):
                sp.dma_start(bia[S * r:S * r + S, :], bias).then_inc(d_bm, 16)
                m = mask[r:r + 1, :]
                sp.dma_start(msk[S * r:S * r + S, :, :],
                             bass.AP(m.tensor, m.offset, [[0, S], [2 * S, PAIRS], [1, S]])).then_inc(d_bm, 16)
            sp.dma_start(wf1[:, :], ffn1).then_inc(d_f1, 16)
            sp.wait_ge(s_T, UNITS)
            sp.dma_start(xs[:, :, D:ROW].bitcast(U32), tok_ids.rearrange("p (i c) -> p i c", c=4)).then_inc(d_tok, 16)
            sp.wait_ge(d_top, 16)
            sp.wait_ge(s_S, UNITS)
            for k in range(TOPK):
                i = sp.value_load(tki[0:1, k:k + 1], min_val=0, max_val=E - 1)
                sp.dma_start(lor[32 * k:32 * k + RANK, :], lora[bass.ds(i, 1), :, :].rearrange("a r n -> (a r) n"))\
                    .then_inc(d_lora, 16)
            sp.wait_ge(s_te, 1)

            def first_row(j):
                return sp.value_load(row0[0:1, j:j + 1], min_val=0, max_val=(ROW_TILES - 1) * P)

            first = [first_row(j) for j in range(EARLY)]
            sp.wait_ge(d_scat, 16 * TILES)
            for j in range(SLOT_TILES):
                if j >= EARLY:
                    first.append(first_row(j))
                sp.dma_start(XS[:, j, :], xs_dram[bass.ds(first[j], P), :]).then_inc(d_xs[j], 16)
            sp.wait_ge(s_S, UNITS)
            sp.wait_ge(s_kt, 2 * CH)
            for h in range(H):
                r = slice(h * DK, (h + 1) * DK)
                sp.dma_start(Kx[r, h % HH, :], KT[r, :]).then_inc(d_kx, 16)
            sp.wait_ge(d_yscat, 16 * SLOT_TILES)
            for a in range(PIECES):
                sp.dma_start(yg[:, piece(a), :], y_dram.rearrange("(i p) d -> p i d", p=P)[:, piece(a), :])\
                    .then_inc(d_yg[a], 16)
            for a in range(PIECES):
                sp.wait_ge(s_fin, a + 1)
                sp.dma_start(out.rearrange("(i p) d -> p i d", p=P)[:, piece(a), :], xres[4][:, piece(a), :])\
                    .then_inc(d_out, 16)
            sp.wait_ge(d_out, 16 * PIECES)

        @block.gpsimd
        def _(pool):
            links = [0]

            def link(ins):
                links[0] += 1
                ins.then_inc(g_chain, 1)
                pool.wait_ge(g_chain, links[0])

            pool.memset(QT[:, :, :], 0.0).then_inc(s_zq, 1)
            pool.memset(nhalf[:, :], -0.5).then_inc(s_nh, 1)
            pool.wait_ge(s_nh, 1)

            def rstd_of(q, a):
                pool.wait_ge(s_ve_, stat_count(q, a))
                w = piece(a)
                pool.tensor_tensor(rstd[:, w], ve[:, w], nhalf[:, w], ALU.pow).then_inc(s_pow, 1)

            def residual_base(layer, c):
                pool.wait_ge(s_bo, layer + 1)
                if layer == 0:
                    pool.wait_ge(d_x[c], 16)
                if layer == 1:
                    pool.wait_ge(s_res, RES_X2 + 2 * c + 2)
                pool.tensor_tensor(xb[:, tiles(c), :], xres[2 * layer][:, tiles(c), :],
                                   mid_bcast(bo[:, :], TPC), ALU.add).then_inc(s_xb, 1)

            pool.memset(Vx[:, 0:HH, :, :], 0.0).then_inc(s_zv, 1)
            for a in (0, 1):
                rstd_of(0, a)
            pool.wait_ge(d_cst, 32)
            for n, w in enumerate((cols(1, TPP * P), cols(1))):
                pool.wait_ge(s_kt, n + 1)
                for h in range(HH):
                    if h == (2, 0)[n]:
                        rstd_of(0, 2 + n)
                    if n == 1 and h == HH // 2:
                        pool.memset(Vx[:, HH:B, :, :], 0.0).then_inc(s_zv, 1)
                    m = cst[:, HM + h:HM + h + 1]
                    pool.tensor_tensor(Kx[:, h, w], KT[:, w],
                                       bass.AP(m.tensor, m.offset, [list(m.ap[0]), [0, w.stop - w.start]]), ALU.mult)\
                        .then_inc(s_kx1, 1)
            for c in range(CH):
                residual_base(0, c)
            for a in range(PIECES):
                rstd_of(1, a)
            pool.wait_ge(d_init, 16)
            pool.wait_ge(d_tok, 16)
            for g, (t0, t1) in enumerate(GROUPS):
                pool.wait_ge(s_slot, g + 1)
                pool.wait_ge(s_xs, g + 1)
                for i in range(t0, t1):
                    pool.indirect_dma_start(out=xs_dram,
                                            out_offset=bass.IndirectOffsetOnAxis(ap=slot[:, i:i + 1], axis=0),
                                            in_=xs[:, i, :], in_offset=None).then_inc(d_scat, 16)
            for j in range(SLOT_TILES):
                pool.wait_ge(s_ys, j + 1)
                pool.indirect_dma_start(out=y_dram,
                                        out_offset=bass.IndirectOffsetOnAxis(ap=XS.bitcast(U32)[:, j, D:D + 1], axis=0),
                                        in_=ys[:, j, :], in_offset=None,
                                        bounds_check=T - 1, oob_is_err=False).then_inc(d_yscat, 16)
            for a in range(PIECES):
                rstd_of(2, a)
            for u in range(UNITS + 5):
                if u < UNITS:
                    U = UNITS + u
                    pool.wait_ge(s_mx, u + 1)
                    pool.wait_ge(s_exp, U - 1)
                    pool.tensor_tensor(Sx[:, u % 2, :].rearrange("p (h k) -> p h k", h=HH),
                                       Sa[:, u % 2, :].rearrange("p (h k) -> p h k", h=HH),
                                       last_bcast(mx[:, u % 4, :], S), ALU.subtract).then_inc(s_sub, 1)
                if u in (4, 6):
                    residual_base(1, u // 2 - 2)
                if u in (9, 13, 17, 20):
                    rstd_of(3, (9, 13, 17, 20).index(u))

        @block.scalar
        def _(act):
            act.dma_start(wat[0][:, :], att0).then_inc(d_att0, 16)
            act.dma_start(cst[:, :], consts).then_inc(d_cst, 16)
            act.dma_start(cstb[:, :].bitcast(mybir.dt.uint16), constb).then_inc(d_cst, 16)
            act.wait_ge(s_zb, 1)
            act.activation(tg[:, :], zb[:, 0:4], ACT.Tanh)

            def k_evac(layer, c):
                act.wait_ge(s_kp, CH * layer + c + 1)
                if layer == 1 and c == 0:
                    act.wait_ge(s_kx0, HH - ACT_HEADS)
                    act.wait_ge(s_kx1, 2 * HH)
                act.activation(KT[:, cols(c)], bank[K_BANK[layer][c]][:, :], ACT.Identity,
                               bias=wat[layer][:, BK:BK + 1]).then_inc(s_kt, 1)

            def normalise(q, a):
                act.wait_ge(s_nmr, stat_count(q, a))
                for i in range(a * TPP + (q + 1) % 2, (a + 1) * TPP):
                    ins = act.activation(xn[:, i, :], xres[q][:, i, :], ACT.Identity,
                                         bias=nmr[:, i:i + 1], scale=rstd[:, i:i + 1])
                ins.then_inc(s_xna, 1)

            def xnT_evac(q, a):
                act.wait_ge(s_xT, PIECES * q + a + 1)
                act.activation(xnT[:, cols(a, TPP * P)], bank[XT_BANK[q][a]][:, 0:TPP * P], ACT.Copy).then_inc(s_xnT, 1)

            def shared_tanh(n):
                act.wait_ge(s_shp, n + 1)
                if n >= 2:
                    act.wait_ge(s_shh, n - 1)
                act.activation(tnh[:, n % 2, :], bank[SH_BANKS[n][0]][:, :], ACT.Tanh, scale=0.5).then_inc(s_sht, 1)

            def v_evac(c, r):
                if r == 0:
                    act.wait_ge(s_zv, c + 1)
                    act.wait_ge(s_vp, c + 1)
                src = bank[V_BANK[0][c]][:, :].rearrange("p (b a e d) -> p b a e d", b=HH, a=4, e=2)
                for e in range(2):
                    o = (2 * e + r) * DK
                    ins = act.activation(Vx[S * r:S * r + S, c * HH:(c + 1) * HH, e::2, o:o + DK],
                                         src[S * r:S * r + S, :, :, e, :], ACT.Copy)
                if r == 1:
                    ins.then_inc(s_ve, 1)

            def score_tanh(g):
                w = slice(*GROUPS[g])
                act.wait_ge(s_lmax, g + 1)
                act.activation(th[:, w], lmax[:, w], ACT.Tanh, scale=0.5).then_inc(s_th, 1)

            def relu1(s):
                act.wait_ge(s_z, s + 1)
                if s >= 2:
                    act.wait_ge(s_h1, s - 1)
                act.activation(r1[:, s % 2, :], bank[2 * (s % 3) + 1][:, :], ACT.Relu).then_inc(s_r1, 1)

            def attention(layer):
                for u in range(UNITS + 1):
                    U = UNITS * layer + u
                    if u < UNITS:
                        act.wait_ge(s_sub, U + 1)
                        if U >= 3:
                            act.wait_ge(s_T, U - 2)
                        act.activation(Pe[:, u % 3, :], Sx[:, u % 2, :], ACT.Exp).then_inc(s_exp, 1)
                    if u >= 1:
                        w = u - 1
                        act.wait_ge(s_T, U)
                        act.activation(PT[:, 4 * (w % 2):4 * (w % 2) + 4, cols(w // 2, P)],
                                       bank3(2 + w % 2, 4), ACT.Copy).then_inc(s_pt, 1)
                    q = 2 * layer + 1
                    if u == 1 - layer:
                        normalise(2 * layer, 3)
                    if u == 0 and layer == 0:
                        xnT_evac(0, 2)
                    if u == 2:
                        xnT_evac(2 * layer, 3)
                    if u in (2, 3, 6, 7) and layer == 0:
                        v_evac(u // 4, u % 2)
                    if u == 11:
                        normalise(q, 0)
                    if u == 14:
                        xnT_evac(q, 0)
                    if u == 15:
                        normalise(q, 1)
                xnT_evac(q, 1)
                if layer == 0:
                    shared_tanh(0)
                    normalise(q, 2)
                    score_tanh(0)
                    xnT_evac(q, 2)
                    shared_tanh(1)
                    normalise(q, 3)
                    xnT_evac(q, 3)
                    score_tanh(1)
                    shared_tanh(2)
                    shared_tanh(3)
                else:
                    relu1(0)
                    normalise(q, 2)
                    relu1(1)
                    xnT_evac(q, 2)
                    normalise(q, 3)
                    xnT_evac(q, 3)

            act.wait_ge(d_att0, 16)
            k_evac(0, 0)
            for a in (0, 1):
                normalise(0, a)
            xnT_evac(0, 0)
            act.wait_ge(d_cst, 32)
            act.wait_ge(s_kt, 1)
            w = cols(0, TPP * P)
            for h in range(HH - ACT_HEADS, HH):
                act.activation(Kx[:, h, w], KT[:, w], ACT.Copy, scale=cst[:, HM + h:HM + h + 1]).then_inc(s_kxa, 1)
            xnT_evac(0, 1)
            k_evac(0, 1)
            act.wait_ge(d_row, 16)
            act.activation(tg[:, :], row[:, GATES:GATES + 4], ACT.Tanh).then_inc(s_tg, 1)
            normalise(0, 2)
            attention(0)
            for c in range(CH):
                k_evac(1, c)
            for j in range(SLOT_TILES + 2):
                if j < SLOT_TILES:
                    act.wait_ge(s_t1, j + 1)
                    if j >= 2:
                        act.wait_ge(s_gu, j - 1)
                    act.activation(xsT[:, j % 2, :], bank[j % 2][:, 0:P], ACT.Copy).then_inc(s_xsT, 1)
                if 1 <= j <= SLOT_TILES:
                    w = j - 1
                    act.wait_ge(s_gu, w + 1)
                    act.wait_ge(s_shh, 4)
                    if w >= 2:
                        act.wait_ge(s_rh, w - 1)
                    act.activation(tnh[:, w % 2, 0:F], bank[2 + w % 2][:, 0:F], ACT.Tanh, scale=0.5).then_inc(s_rt, 1)
                if j >= 2:
                    w = j - 2
                    act.wait_ge(s_t2, w + 1)
                    if w >= 2:
                        act.wait_ge(s_y, w - 1)
                    act.activation(hrT[:, w % 2, :], bank[4 + w % 2][:, 0:F], ACT.Copy).then_inc(s_hT, 1)
            for a in (0, 1):
                normalise(2, a)
                xnT_evac(2, a)
            normalise(2, 2)
            xnT_evac(2, 2)
            attention(1)
            for s in range(2, CH * FB1):
                relu1(s)

        @block.vector
        def _(dve):
            links = [0]

            def link(ins):
                links[0] += 1
                ins.then_inc(v_chain, 1)
                dve.wait_ge(v_chain, links[0])

            def stats(q, a):
                w = range(a * TPP, (a + 1) * TPP)
                for i in w:
                    ins = dve.bn_stats(st[:, i, :], xres[q][:, i, :])
                link(ins)
                for i in w:
                    ins = dve.bn_aggr(mv[:, i, :], st[:, i, :])
                link(ins)
                w = slice(w[0], w[-1] + 1)
                dve.tensor_scalar(ve[:, w], mv[:, w, 1], EPS, None, ALU.add).then_inc(s_ve_, 1)

            def mean_rstd(q, a):
                dve.wait_ge(s_pow, stat_count(q, a))
                w = piece(a)
                dve.scalar_tensor_tensor(out=nmr[:, w], in0=mv[:, w, 0], scalar=-1.0,
                                         in1=rstd[:, w], op0=ALU.mult, op1=ALU.mult).then_inc(s_nmr, 1)

            def normalise(q, a):
                mean_rstd(q, a)
                i = a * TPP
                dve.tensor_scalar(xn[:, i, :], xres[q][:, i, :], mv[:, i, 0:1], rstd[:, i:i + 1],
                                  ALU.subtract, ALU.mult).then_inc(s_xnv, 1)

            def bias_cols(layer):
                dve.tensor_scalar(bvb[:, :], ident, 0.0, wat[layer][:, BV:BV + 1], ALU.mult, ALU.add).then_inc(s_bvb, 1)

            def bias_out(layer):
                dve.wait_ge(s_ob, layer + 1)
                link(dve.tensor_tensor(bo[:, :], bank[OB_BANK[layer]][:, 0:D], row[:, (BO0, BO1)[layer]:(BO0, BO1)[layer] + D],
                                       ALU.add))
                dve.tensor_scalar(bo[:, :], bo[:, :], tg[:, layer:layer + 1], None, ALU.mult).then_inc(s_bo, 1)

            def v_evac(c):
                dve.wait_ge(s_vp, CH + c + 1)
                src = bank[V_BANK[1][c]][:, :].rearrange("p (b a e d) -> p b a e d", b=HH, a=4, e=2)
                for r in range(2):
                    for e in range(2):
                        o = (2 * e + r) * DK
                        ins = dve.tensor_copy(
                            Vx[S * r:S * r + S, c * HH:(c + 1) * HH, e::2, o:o + DK], src[S * r:S * r + S, :, :, e, :])
                ins.then_inc(s_ve, 1)

            def q_evac(layer, a):
                dve.wait_ge(s_qp, PIECES * layer + a + 1)
                for hh in range(2):
                    w = slice(hh * P // 2, (hh + 1) * P // 2)
                    dve.tensor_scalar(QT[w, hh, cols(a, TPP * P)], bank[Q_BANK[layer][a]][w, 0:TPP * P],
                                      wat[layer][w, BQ:BQ + 1], SCALE, ALU.add, ALU.mult).then_inc(s_qt, 1)

            def unit(layer, u):
                U = UNITS * layer + u
                ps = bank3(u % 2, HH)
                dve.wait_ge(s_S, U + 1)
                if layer == 0:
                    link(dve.tensor_reduce(mx[:, u % 4, :], ps, AX.X, ALU.max))
                    if u >= 2:
                        dve.wait_ge(s_exp, U - 1)
                    dve.tensor_tensor(Sx[:, u % 2, :].rearrange("p (h k) -> p h k", h=HH), ps,
                                      last_bcast(mx[:, u % 4, :], S), ALU.subtract).then_inc(s_sub, 1)
                else:
                    sa = Sa[:, u % 2, :].rearrange("p (h k) -> p h k", h=HH)
                    if u >= 2:
                        dve.wait_ge(s_sub, U - 1)
                    dve.tensor_tensor(sa, ps, mid_bcast(bm[:, u // 2, :], HH), ALU.add).then_inc(s_add, 1)
                    dve.wait_ge(s_add, u + 1)
                    dve.tensor_reduce(mx[:, u % 4, :], sa, AX.X, ALU.max).then_inc(s_mx, 1)

            def norm(layer, bp):
                dve.wait_ge(s_av, PAIRS * layer + bp + 1)
                link(dve.reciprocal(oT[:, cols(bp, P)], bank[4 + bp % 2][:, P:2 * P]))
                dve.tensor_tensor(oT[:, cols(bp, P)], bank[4 + bp % 2][:, 0:P], oT[:, cols(bp, P)], ALU.mult)\
                    .then_inc(s_oT, 1)

            def residual(layer, a):
                dve.wait_ge(s_op, PAIRS * layer + TPP * (a + 1))
                dve.wait_ge(s_xb, CH * layer + a // 2 + 1)
                dve.scalar_tensor_tensor(out=xres[2 * layer + 1][:, piece(a), :],
                                         in0=bank[6][:, 0:TPP * D].rearrange("p (i d) -> p i d", i=TPP),
                                         scalar=tg[:, layer:layer + 1], in1=xb[:, piece(a), :],
                                         op0=ALU.mult, op1=ALU.add).then_inc(s_res, 1)
                dve.wait_ge(s_res, (0, RES_L1)[layer] + a + 1)
                stats(2 * layer + 1, a)

            def pick(g):
                t0, t1 = GROUPS[g]
                w, n = slice(t0, t1), t1 - t0
                lg = bank[LG_BANK[g]][:, 0:n * E].rearrange("p (i e) -> p i e", e=E)
                dve.wait_ge(s_lg, g + 1)
                dve.tensor_reduce(lmax[:, w], lg, AX.X, ALU.max).then_inc(s_lmax, 1)
                dve.wait_ge(s_lmax, g + 1)
                link(dve.tensor_tensor(eq[:, w, :], lg, last_bcast(lmax[:, w], E), ALU.is_equal))
                link(dve.tensor_tensor(wv[:, w, :], eq[:, w, :], mid_bcast(cst[:, W8:W8 + E], n), ALU.mult))
                link(dve.tensor_reduce(fmx[:, w], wv[:, w, :], AX.X, ALU.max))
                dve.tensor_tensor(oh[:, w, :], wv[:, w, :], last_bcast(fmx[:, w], E), ALU.is_equal).then_inc(s_oh, 1)
                dve.wait_ge(s_th, g + 1)
                link(dve.tensor_scalar(score[:, w], th[:, w], 0.5, 0.5, ALU.mult, ALU.add))
                dve.tensor_tensor(xs[:, w, 0:D], xn[:, w, :], last_bcast(score[:, w], D), ALU.mult).then_inc(s_xs, 1)

            def place(g):
                t0, t1 = GROUPS[g]
                w, n = slice(t0, t1), t1 - t0
                pre = bank[LG_BANK[g]][:, 64:64 + n * E].rearrange("p (i e) -> p i e", e=E)
                dve.wait_ge(s_pre, g + 1)
                link(dve.tensor_tensor(sl[:, w, :], pre, mid_bcast(cst[:, REG:REG + E], n), ALU.add))
                link(dve.tensor_tensor(slo[:, w, :], sl[:, w, :], oh[:, w, :], ALU.mult))
                link(dve.tensor_reduce(slotf[:, w], slo[:, w, :], AX.X, ALU.add))
                dve.tensor_copy(slot[:, w], slotf[:, w]).then_inc(s_slot, 1)

            def tile_table():
                cnt = bank[LG_BANK[-1]][0:1, 128:128 + E]
                link(dve.tensor_tensor(cmp8[0:1, :, :], last_bcast(cnt, 8), mid_bcast(cst[0:1, THR:THR + 8], E), ALU.is_gt))
                link(dve.tensor_reduce(nt[0:1, :], cmp8[0:1, :, :], AX.X, ALU.add))
                link(dve.tensor_tensor(nt8[0:1, :, :], mid_bcast(nt[0:1, :], E),
                                       cst[0:1, TRI8:TRI8 + 64].rearrange("p (a b) -> p a b", a=E), ALU.mult))
                link(dve.tensor_reduce(endt[0:1, :], nt8[0:1, :, :], AX.X, ALU.add))
                link(dve.tensor_tensor(tej[:, :, :], mid_bcast(endt[0:1, :], SLOT_TILES),
                                       last_bcast(cst[0:1, JT:JT + SLOT_TILES], E), ALU.is_le))
                link(dve.tensor_reduce(tef[:, :], tej[:, :, :], AX.X, ALU.add))
                link(dve.tensor_tensor(tbj[:, :, :], tej[:, :, :], mid_bcast(nt[0:1, :], SLOT_TILES), ALU.mult))
                link(dve.tensor_reduce(tbf[:, :], tbj[:, :, :], AX.X, ALU.add))
                link(dve.tensor_scalar(teo[:, :], tef[:, :], float(E - 1), float(2 * D), ALU.min, ALU.mult))
                link(dve.scalar_tensor_tensor(out=row0f[:, :], in0=tbf[:, :], scalar=-float(P),
                                              in1=cst[0:1, JP:JP + SLOT_TILES], op0=ALU.mult, op1=ALU.add))
                dve.scalar_tensor_tensor(out=row0[:, :], in0=tef[:, :], scalar=float(T),
                                         in1=row0f[:, :], op0=ALU.mult, op1=ALU.add).then_inc(s_te, 1)

            def attention(layer, step):
                q = 2 * layer + 1
                for bp in range(PAIRS):
                    unit(layer, 2 * bp)
                    if bp == 0 and layer == 0:
                        stats(0, 3)
                    if bp == 0 and layer == 1:
                        normalise(2, 3)
                    if bp in (1, 2):
                        q_evac(layer, bp + 1)
                    if bp in (5, 7):
                        mean_rstd(q, (bp - 5) // 2)
                    unit(layer, 2 * bp + 1)
                    if bp == 0:
                        q_evac(layer, 1)
                        if layer == 0:
                            normalise(0, 3)
                            dve.wait_ge(s_tg, 1)
                            dve.wait_ge(d_row, 16)
                            bias_out(0)
                    if bp >= 2:
                        norm(layer, bp - 2)
                    if bp in (4, 6):
                        residual(layer, (bp - 4) // 2)
                norm(layer, 6)
                residual(layer, 2)
                norm(layer, 7)
                mean_rstd(q, 2)
                if layer == 0:
                    pick(0)
                else:
                    step(0)
                residual(layer, 3)
                if layer == 0:
                    place(0)
                mean_rstd(q, 3)
                if layer == 0:
                    step(0)
                step(1)
                if layer == 0:
                    pick(1)
                    place(1)
                    tile_table()
                    step(2)
                    step(3)

            def shared_step(n):
                c, f = n // 2, n % 2
                g, up = SH_BANKS[n]
                dve.wait_ge(s_sht, n + 1)
                link(dve.scalar_tensor_tensor(out=gac[:, n % 2, :], in0=tnh[:, n % 2, :], scalar=1.0,
                                              in1=bank[g][:, :], op0=ALU.add, op1=ALU.mult))
                dve.scalar_tensor_tensor(out=hsT[:, f, cols(c)], in0=gac[:, n % 2, :], scalar=0.5,
                                         in1=bank[up][:, :], op0=ALU.mult, op1=ALU.mult).then_inc(s_shh, 1)

            def ffn1_step(s):
                c, f = s // FB1, s % FB1
                dve.wait_ge(s_z, s + 1)
                link(dve.tensor_scalar(r0[:, s % 2, :], bank[2 * (s % 3)][:, :], 0.0, row[:, TOPV:TOPV + 1],
                                       ALU.max, ALU.mult))
                dve.wait_ge(s_r1, s + 1)
                dve.scalar_tensor_tensor(out=h1T[:, f, cols(c)], in0=r1[:, s % 2, :], scalar=row[:, TOPV + 1:TOPV + 2],
                                         in1=r0[:, s % 2, :], op0=ALU.mult, op1=ALU.add).then_inc(s_h1, 1)

            dve.memset(zb[:, :], 0.0).then_inc(s_zb, 1)
            dve.wait_ge(d_x[0], 16)
            for a in (0, 1):
                stats(0, a)
            for a in (0, 1):
                normalise(0, a)
            dve.wait_ge(d_cst, 32)
            dve.wait_ge(s_kt, 1)
            w = cols(0, TPP * P)
            for h in range(HH - ACT_HEADS):
                dve.tensor_scalar(Kx[:, h, w], KT[:, w], cst[:, HM + h:HM + h + 1], None, ALU.mult).then_inc(s_kx0, 1)
            dve.wait_ge(s_zq, 1)
            dve.wait_ge(d_att0, 16)
            bias_cols(0)
            q_evac(0, 0)
            dve.wait_ge(d_x[1], 16)
            stats(0, 2)
            normalise(0, 2)
            attention(0, shared_step)

            for c in range(CH):
                dve.wait_ge(s_sdn, c + 1)
                dve.scalar_tensor_tensor(out=xb[:, tiles(c), :], in0=bank3(SD_BANK[c], TPC), scalar=tg[:, 2:3],
                                         in1=xres[1][:, tiles(c), :], op0=ALU.mult, op1=ALU.add).then_inc(s_shr, 1)
            dve.wait_ge(d_att1, 16)
            bias_cols(1)
            dve.wait_ge(d_bm, 64)
            link(dve.tensor_scalar(bm[:, :, :], msk[:, :, :], NEG, None, ALU.mult))
            link(dve.tensor_tensor(bm[:, :, :], bm[:, :, :], mid_bcast(bia[:, :], PAIRS), ALU.add))
            for j in range(SLOT_TILES + 2):
                if j < SLOT_TILES:
                    g = bank[2 + j % 2]
                    dve.wait_ge(s_rt, j + 1)
                    link(dve.scalar_tensor_tensor(out=gac[:, j % 2, 0:F], in0=tnh[:, j % 2, 0:F], scalar=1.0,
                                                  in1=g[:, 0:F], op0=ALU.add, op1=ALU.mult))
                    if j >= 2:
                        dve.wait_ge(s_t2, j - 1)
                    dve.scalar_tensor_tensor(out=hr[:, j % 2, :], in0=gac[:, j % 2, 0:F], scalar=0.5,
                                             in1=g[:, F:2 * F], op0=ALU.mult, op1=ALU.mult).then_inc(s_rh, 1)
                if j >= 2:
                    w = j - 2
                    dve.wait_ge(s_y, w + 1)
                    dve.tensor_copy(ys[:, w, :], bank[6 + w % 2][:, 0:D]).then_inc(s_ys, 1)
            for c in range(CH):
                v_evac(c)
            bias_out(1)
            for k in range(TOPK):
                dve.wait_ge(s_wl, k + 1)
                if k == 0:
                    dve.wait_ge(d_f1, 16)
                dve.tensor_tensor(weff[:, k, :], bank[4 + k][:, :], wf1[:, 0:F1], ALU.add).then_inc(s_we, 1)
            for a in range(PIECES):
                dve.wait_ge(d_yg[a], 16)
                dve.scalar_tensor_tensor(out=xres[2][:, piece(a), :], in0=yg[:, piece(a), :], scalar=tg[:, 2:3],
                                         in1=xb[:, piece(a), :], op0=ALU.mult, op1=ALU.add).then_inc(s_res, 1)
                dve.wait_ge(s_res, RES_X2 + a + 1)
                if a >= 1:
                    normalise(2, a - 1)
                if a == 3:
                    q_evac(1, 0)
                stats(2, a)
            attention(1, ffn1_step)
            for s in range(2, CH * FB1):
                ffn1_step(s)
            for a in range(PIECES):
                dve.wait_ge(s_dn, a + 1)
                dve.scalar_tensor_tensor(out=xres[4][:, piece(a), :],
                                         in0=bank[DN_BANK[a]][:, 0:TPP * D].rearrange("p (i d) -> p i d", i=TPP),
                                         scalar=tg[:, 3:4], in1=xres[3][:, piece(a), :],
                                         op0=ALU.mult, op1=ALU.add).then_inc(s_fin, 1)

        @block.tensor
        def _(pe):
            def mm(o, l, r, first=True, last=True, **k):
                return pe.matmul(o, l, r, start=first, stop=last, **k)

            def keep_warm(b, n):
                for _ in range(n):
                    mm(bank[b][0:32, :].rearrange("p (a c) -> p a c", c=32), zb[:, :], mid_bcast(zb[:, :], TC // 32))

            def k_proj(layer):
                for c in range(CH):
                    pe.wait_ge(d_ctx[c], 16)
                    mm(bank[K_BANK[layer][c]][:, :], wat[layer][:, WK:WK + D], ctxT[:, cols(c)]).then_inc(s_kp, 1)

            def v_proj(layer, c):
                wvt = wat[layer][:, WV:WV + D].rearrange("p (a r d) -> p r a d", r=2, d=DK)
                for n in range(HH):
                    b = c * HH + n
                    for r in range(2):
                        o = bank[V_BANK[layer][c]][S * r:S * r + S, n * S:(n + 1) * S]
                        ins = mm(o.rearrange("p (a d) -> p a d", d=DK), ctxT[:, b * S:(b + 1) * S], wvt[:, r])
                ins.then_inc(s_vp, 1)

            def out_bias(layer):
                pe.wait_ge(s_bvb, layer + 1)
                mm(bank[OB_BANK[layer]][:, 0:D], bvb[:, :], wat[layer][:, WO:WO + D]).then_inc(s_ob, 1)

            def xn_transpose(q, a):
                n = PIECES * q + a + 1
                if q % 2:
                    if a:
                        pe.wait_ge(s_xnT, n - 1)
                    if q == 1 and a == 3:
                        keep_warm(XT_BANK[q][a], 8)
                else:
                    pe.wait_ge(s_xnv, PIECES * (q // 2) + a + 1)
                pe.wait_ge(s_xna, n)
                for k in range(TPP):
                    ins = pe.transpose(bank[XT_BANK[q][a]][:, k * P:(k + 1) * P], xn[:, a * TPP + k, :], ident)
                ins.then_inc(s_xT, 1)

            def q_proj(layer, a):
                pe.wait_ge(s_xnT, PIECES * 2 * layer + a + 1)
                mm(bank[Q_BANK[layer][a]][:, 0:TPP * P], wat[layer][:, WQ:WQ + D], xnT[:, cols(a, TPP * P)])\
                    .then_inc(s_qp, 1)

            def scores(layer, u):
                U = UNITS * layer + u
                bp, hh = u // 2, u % 2
                if u >= 2:
                    if layer == 0:
                        pe.wait_ge(s_sub, U - 1)
                    else:
                        pe.wait_ge(s_add, u - 1)
                for r in range(2):
                    b = 2 * bp + r
                    ins = mm(bank[u % 2][S * r:S * r + S, :].rearrange("p (h k) -> p h k", h=HH),
                             QT[:, hh, b * S:(b + 1) * S], Kx[:, :, b * S:(b + 1) * S])
                ins.then_inc(s_S, 1)

            def transposes(layer, u):
                U = UNITS * layer + u
                if u == 1:
                    pe.wait_ge(s_qt, 2 * (PIECES * layer + 2))
                pe.wait_ge(s_exp, U + 1)
                if U >= 2:
                    pe.wait_ge(s_pt, U - 1)
                for m in range(4):
                    ins = pe.transpose(bank[2 + u % 2][:, m * P:(m + 1) * P], Pe[:, u % 3, m * P:(m + 1) * P], ident)
                ins.then_inc(s_T, 1)

            def values(layer, bp):
                pe.wait_ge(s_pt, UNITS * layer + 2 * bp + 2)
                pe.wait_ge(s_ve, CH * layer + bp // (PAIRS // CH) + 1)
                if layer == 0 and bp < 2:
                    pe.wait_ge(s_qt, 2 * (3 + bp))
                if bp >= 2:
                    pe.wait_ge(s_oT, PAIRS * layer + bp - 1)
                o = bank[4 + bp % 2]
                for e in range(2):
                    for g in range(4):
                        a = 2 * g + e
                        mm(o[32 * g:32 * g + 32, P:2 * P], onesx[:, e, :],
                           PT[:, a, bp * P:(bp + 1) * P], first=(e == 0), last=(e == 1), tile_position=(0, 32 * g))
                for r in range(2):
                    b = 2 * bp + r
                    for e in range(2):
                        for g in range(4):
                            a = 2 * g + e
                            ins = mm(o[32 * g:32 * g + 32, S * r:S * r + S], Vx[:, b, a, :],
                                     PT[:, a, b * S:(b + 1) * S], first=(e == 0), last=(e == 1), tile_position=(0, 32 * g))
                ins.then_inc(s_av, 1)

            def out_proj(layer, bp):
                pe.wait_ge(s_oT, PAIRS * layer + bp + 1)
                if layer == 1 and bp == 0:
                    pe.wait_ge(s_qt, 2 * (PIECES + 3))
                if bp % TPP == 0 and bp:
                    pe.wait_ge(s_res, (0, RES_L1)[layer] + bp // TPP)
                k = bp % TPP
                mm(bank[6][:, k * D:(k + 1) * D], oT[:, bp * P:(bp + 1) * P], wat[layer][:, WO:WO + D]).then_inc(s_op, 1)

            def attention(layer, step):
                q = 2 * layer + 1
                if layer == 1:
                    pe.wait_ge(d_kx, 16 * H)
                    pe.wait_ge(s_ve, 2 * CH)
                for bp in range(PAIRS + 1):
                    if bp == 2:
                        xn_transpose(2 * layer, 3)
                    if bp == 3 and layer == 0:
                        pe.wait_ge(s_bo, 1)
                        v_proj(0, 1)
                    if bp % TPP == 0 and bp < PAIRS:
                        pe.wait_ge(s_qt, 2 * (PIECES * layer + bp // TPP + 1))
                    if layer == 0:
                        if bp == 0:
                            pe.wait_ge(s_kx0, HH - ACT_HEADS)
                            pe.wait_ge(s_kxa, ACT_HEADS)
                            pe.wait_ge(s_kt, CH)
                        if bp == 2:
                            pe.wait_ge(s_kx1, HH)
                        if bp == 4:
                            pe.wait_ge(s_kx1, 2 * HH)
                    for hh in range(2):
                        if bp < PAIRS:
                            scores(layer, 2 * bp + hh)
                        if bp == 0 and hh == 1:
                            if layer == 0:
                                v_proj(0, 0)
                                out_bias(0)
                            if layer == 1:
                                keep_warm(XT_BANK[2][2], 2)
                            xn_transpose(2 * layer, 2)
                            q_proj(layer, 2)
                        if bp == PAIRS and hh == 1:
                            pe.wait_ge(s_xnT, PIECES * q + 1)
                            keep_warm(XT_BANK[q][0], 3)
                        if bp >= 1:
                            transposes(layer, 2 * bp - 2 + hh)
                        if bp == 2 and hh == 0:
                            q_proj(layer, 3)
                    if bp >= 2:
                        values(layer, bp - 2)
                    if bp >= 3:
                        out_proj(layer, bp - 3)
                    if bp == 7:
                        xn_transpose(q, 0)
                xn_transpose(q, 1)
                values(layer, 7)
                out_proj(layer, 6)
                if layer == 0:
                    logits(0)
                step(0)
                if layer == 1:
                    step(1)
                out_proj(layer, 7)
                xn_transpose(q, 2)

            pe.wait_ge(s_zb, 1)
            keep_warm(2, 9)
            pe.wait_ge(d_att0, 16)
            k_proj(0)
            pe.wait_ge(d_cst, 32)
            for a in (0, 1):
                xn_transpose(0, a)
                q_proj(0, a)

            def shared_up(n):
                c, f = n // 2, n % 2
                if n == 0:
                    pe.wait_ge(d_sh, 16)
                    pe.wait_ge(s_sub, UNITS)
                if n == 1:
                    pe.wait_ge(s_oT, PAIRS)
                if n == 2:
                    pe.wait_ge(s_shh, 1)
                if n == 3:
                    pe.wait_ge(s_xnT, 2 * PIECES)
                pe.wait_ge(s_xnT, PIECES + 2 * c + 2)
                for k in range(2):
                    ins = mm(bank[SH_BANKS[n][k]][:, :], wsh[:, k * F + f * P:k * F + (f + 1) * P], xnT[:, cols(c)])
                ins.then_inc(s_shp, 1)

            def ffn1_up(s):
                c, f = s // FB1, s % FB1
                pe.wait_ge(s_xnT, PIECES * 3 + 2 * c + 2)
                if s == 0:
                    pe.wait_ge(s_we, TOPK)
                    pe.wait_ge(s_add, UNITS)
                if s == 1:
                    pe.wait_ge(s_pt, 2 * UNITS)
                if s == 2:
                    pe.wait_ge(s_oT, 2 * PAIRS)
                if s >= 3:
                    pe.wait_ge(s_h1, s - 2)
                for k in range(TOPK):
                    ins = mm(bank[2 * (s % 3) + k][:, :], weff[:, k, f * P:(f + 1) * P], xnT[:, cols(c)])
                ins.then_inc(s_z, 1)

            def logits(g):
                t0, t1 = GROUPS[g]
                if g == 0:
                    pe.wait_ge(s_pt, UNITS)
                if g == 1:
                    pe.wait_ge(s_oT, PAIRS - 1)
                pe.wait_ge(s_xnT, PIECES + t1 // TPP)
                for i in range(t0, t1):
                    ins = mm(bank[LG_BANK[g]][:, (i - t0) * E:(i - t0 + 1) * E], xnT[:, i * P:(i + 1) * P],
                             wat[0][:, WGATE:WGATE + E])
                ins.then_inc(s_lg, 1)

            def ranks(g):
                t0, t1 = GROUPS[g]
                n = t1 - t0
                flat = lambda ap: ap.rearrange("p i e -> p (i e)")
                pre = bank[LG_BANK[g]][:, 64:64 + n * E]
                pe.wait_ge(s_oh, g + 1)
                ins = mm(pre, tri, flat(oh[:, t0:t1, :]), skip_group_check=True)
                for s in range(1, n):
                    ins = mm(pre[:, s * E:n * E], ones_bf, flat(oh[:, t0:t1 - s, :]), first=False, skip_group_check=True)
                for i in range(t0):
                    ins = mm(pre.rearrange("p (i e) -> p i e", e=E), ones_bf, mid_bcast(oh[:, i, :], n),
                             first=False, skip_group_check=True)
                if g == len(GROUPS) - 1:
                    for i in range(TILES):
                        ins = mm(bank[LG_BANK[g]][:, 128:128 + E], ones_bf, oh[:, i, :], first=(i == 0), last=(i == TILES - 1))
                ins.then_inc(s_pre, 1)

            attention(0, shared_up)
            ranks(0)
            shared_up(1)
            xn_transpose(1, 3)
            logits(1)
            keep_warm(7, 5)
            ranks(1)
            shared_up(2)
            shared_up(3)
            for c in range(CH):
                if c == 1:
                    pe.wait_ge(d_att1, 16)
                    pe.wait_ge(s_shh, 3)
                    k_proj(1)
                pe.wait_ge(s_shh, (2, 4)[c])
                for i in range(TPC):
                    t = c * TPC + i
                    for f in range(2):
                        ins = mm(bank[SD_BANK[c]][:, i * D:(i + 1) * D], hsT[:, f, t * P:(t + 1) * P],
                                 wsh[:, 2 * F + f * D:2 * F + (f + 1) * D], first=(f == 0), last=(f == 1))
                ins.then_inc(s_sdn, 1)
            pe.wait_ge(d_rgu, 16)
            pe.wait_ge(d_rdn, 16)
            pe.wait_ge(s_te, 1)
            pe.wait_ge(s_kt, 2 * CH)
            keep_warm(0, 3)
            first_col = {}
            for j in range(SLOT_TILES + 3):
                if j < SLOT_TILES:
                    pe.wait_ge(d_xs[j], 16)
                    if j >= 2:
                        pe.wait_ge(s_xsT, j - 1)
                    pe.transpose(bank[j % 2][:, 0:P], XS[:, j, 0:D], ident).then_inc(s_t1, 1)
                if 1 <= j <= SLOT_TILES:
                    w = j - 1
                    e = pe.value_load(teo[0:1, w:w + 1], min_val=0, max_val=(E - 1) * 2 * D)
                    first_col[w] = e
                    pe.wait_ge(s_xsT, w + 1)
                    if w == 1:
                        pe.wait_ge(s_shr, CH)
                    if w >= 2:
                        pe.wait_ge(s_rh, w - 1)
                    mm(bank[2 + w % 2][:, :], xsT[:, w % 2, :], wgu[:, bass.ds(e * 2, 2 * F)]).then_inc(s_gu, 1)
                if 2 <= j <= SLOT_TILES + 1:
                    w = j - 2
                    pe.wait_ge(s_rh, w + 1)
                    if w >= 2:
                        pe.wait_ge(s_hT, w - 1)
                    for f in range(2):
                        ins = pe.transpose(bank[4 + w % 2][:, f * P:(f + 1) * P], hr[:, w % 2, f * P:(f + 1) * P], ident)
                    ins.then_inc(s_t2, 1)
                if j >= 3:
                    w = j - 3
                    e = first_col[w]
                    pe.wait_ge(s_hT, w + 1)
                    if w >= 2:
                        pe.wait_ge(s_ys, w - 1)
                    for f in range(2):
                        ins = mm(bank[6 + w % 2][:, 0:D], hrT[:, w % 2, f * P:(f + 1) * P],
                                 wdn[:, bass.ds(e + f * D, D)], first=(f == 0), last=(f == 1))
                    ins.then_inc(s_y, 1)
            for c in range(CH):
                v_proj(1, c)
            out_bias(1)
            pe.wait_ge(d_lora, 32)
            pe.wait_ge(s_hT, SLOT_TILES)
            for k in range(TOPK):
                r = slice(32 * k, 32 * k + RANK)
                mm(bank[4 + k][:, :], lor[r, 0:D], lor[r, D:D + F1]).then_inc(s_wl, 1)

            pe.wait_ge(s_bo, 2)
            keep_warm(2, 16)
            for a in (0, 1):
                xn_transpose(2, a)
                keep_warm(6, 2)
                q_proj(1, a)
                keep_warm(6, 2)
            attention(1, ffn1_up)
            ffn1_up(2)
            ffn1_up(3)
            xn_transpose(3, 3)
            for s in range(FB1, CH * FB1):
                ffn1_up(s)
            for a in range(PIECES):
                pe.wait_ge(s_h1, (a // 2 + 1) * FB1)
                for i in range(TPP):
                    t = a * TPP + i
                    for f in range(FB1):
                        ins = mm(bank[DN_BANK[a]][:, i * D:(i + 1) * D], h1T[:, f, t * P:(t + 1) * P],
                                 wf1[:, F1 + f * D:F1 + (f + 1) * D], first=(f == 0), last=(f == FB1 - 1))
                ins.then_inc(s_dn, 1)


_ORDER = ["x_in", "ctx_in", "att0", "att1", "consts", "constb", "rows", "shared", "rgu", "rdn", "ffn1", "lora",
          "topi", "bias", "mask", "tok_ids", "empty_in"]


def pack(a):
    import numpy as np

    def col(v):
        return v.reshape(-1, 1)

    wi, bi = a["L1_xattn_in_proj_w"], a["L1_xattn_in_proj_b"]
    consts = np.zeros((P, CONST_COLS), np.float32)
    consts[:, ID:ID + P] = np.eye(P)
    for p in range(P):
        for e in range(2):
            o = ONESX + 32 * e + (2 * e + p // S) * DK
            consts[p, o:o + DK] = 1.0
    consts[:, W8:W8 + E] = np.arange(E, 0, -1)
    consts[:, REG:REG + E] = np.arange(E) * T
    consts[:, JP:JP + 16] = np.arange(16) * P
    consts[:, THR:THR + 8] = np.arange(8) * P
    consts[:, TRI8:TRI8 + 64] = np.tril(np.ones((E, E))).reshape(-1)
    consts[:, JT:JT + 16] = np.arange(16)
    consts[np.arange(P), HM + np.arange(P) % (P // 2) // DK] = 1.0
    one = 0x3F80
    constb = np.full((P, 2 * P), one, np.uint16)
    constb[:, 0:P] = np.triu(np.ones((P, P)), 1).astype(np.uint16) * one
    tok = np.zeros((P, TILES, 4), np.uint32)
    tok[:, :, 0] = np.arange(TILES)[None, :] * P + np.arange(P)[:, None]
    init = np.zeros((P, ROW), np.uint32)
    init[:, D] = 4 * T + np.arange(P)
    pad = np.zeros((D, E), np.float32)
    return {
        "x_in": a["x"].reshape(T, D),
        "ctx_in": a["ctx_1024"].reshape(T, D).T,
        "att0": np.concatenate([a["L0_xattn_Wk"].T, a["L0_xattn_Wv"].T, col(a["L0_xattn_bk"]), col(a["L0_xattn_bv"]),
                                col(a["L0_xattn_bq"]), a["L0_xattn_Wq"].T, a["L0_xattn_Wo"].T,
                                a["L0_ffn_gate_w"].T], 1),
        "att1": np.concatenate([wi[D:2 * D].T, wi[2 * D:].T, col(bi[D:2 * D]), col(bi[2 * D:]), col(bi[:D]),
                                wi[:D].T, a["L1_xattn_out_proj_w"].T, pad], 1),
        "consts": consts,
        "constb": constb,
        "rows": np.concatenate([a["L0_xattn_bo"], a["L1_xattn_out_proj_b"], a["g_xattn"], a["g_ffn"],
                                a["L1_ffn_top_k_values"]]).reshape(1, -1),
        "shared": np.concatenate([a["L0_ffn_shared_gate"].T, a["L0_ffn_shared_up"].T,
                                  a["L0_ffn_shared_down"].T.reshape(2, P, D).transpose(1, 0, 2).reshape(P, 2 * D)], 1),
        "rgu": np.stack([a["L0_ffn_r_gate"].transpose(2, 0, 1), a["L0_ffn_r_up"].transpose(2, 0, 1)], 2)
                 .reshape(D, E * 2 * F),
        "rdn": a["L0_ffn_r_down"].transpose(2, 0, 1).reshape(2, P, E, D).transpose(1, 2, 0, 3).reshape(P, E * 2 * D),
        "ffn1": np.concatenate([a["L1_ffn_wi_w"].T,
                                a["L1_ffn_wo_w"].T.reshape(FB1, P, D).transpose(1, 0, 2).reshape(P, F1)], 1),
        "lora": np.concatenate([a["L1_ffn_lora_As"], a["L1_ffn_lora_Bs"].transpose(0, 2, 1)], 2),
        "topi": a["L1_ffn_top_k_indices"].reshape(1, TOPK),
        "bias": a["fside_1xSxS2_0"][0],
        "mask": a["mask_BxS2_bk0"],
        "tok_ids": tok.reshape(P, TILES * 4),
        "empty_in": init.view(np.float32),
    }


def kernel(**inputs):
    import numpy as _np
    import concourse.bacc as _bacc
    from concourse import mybir as _mybir
    from concourse.bass_utils import run_bass_kernel_spmd as _run

    nc = _bacc.Bacc("TRN2", target_bir_lowering=False, num_devices=1)
    packed = pack({k: _np.asarray(v) for k, v in inputs.items()})
    arrays, args = {}, []
    for name in _ORDER:
        a = _np.ascontiguousarray(packed[name])
        arrays[name] = a
        args.append(nc.dram_tensor(name, a.shape, _mybir.dt.from_np(a.dtype), kind="ExternalInput").ap())
    out = nc.dram_tensor("out", (T, D), F32, kind="ExternalOutput").ap()
    build(nc, *args, out)
    r = _run(nc, [arrays], core_ids=[0])
    return r.results[0]["out"].reshape(B, S, D)
```
